# Optimizing a Trainium2 kernel written in Bass

```python
import numpy as np
import jax
import jax.numpy as jnp

def _softmax(x, axis=-1):
    return jax.nn.softmax(x, axis=axis)

def _gelu(x):
    return jax.nn.gelu(x, approximate=True)

def _silu(x):
    return jax.nn.silu(x)

def _sigmoid(x):
    return jax.nn.sigmoid(x)

def _layernorm(x, axis=-1, eps=1e-05):
    m = jnp.mean(x, axis=axis, keepdims=True)
    v = jnp.var(x, axis=axis, keepdims=True)
    return (x - m) / jnp.sqrt(v + eps)

def _scatter_add(tgt, idx, src, axis=0):
    return tgt.at[idx].add(src)

def _segment_sum(src, seg, n):
    return jax.ops.segment_sum(src, seg, n)
kernel_name = 'mk_adaln_d2_jaxref_r8_fe2360'

def setup_inputs(seed: int=0):
    np.random.seed(seed)
    _w = jnp.asarray

    def _L0_attn_setup():
        import jax, jax.numpy as jnp
        import numpy as np
        DIM = 128
        NUM_HEADS = 16
        HEAD_DIM = DIM // NUM_HEADS
        key = jax.random.key(seed)
        k1, k2, k3, k4 = jax.random.split(key, 4)
        x = jax.random.normal(k1, (4, 512, DIM), dtype=jnp.float32)
        w_qkv = jax.random.normal(k2, (3 * DIM, DIM), dtype=jnp.float32) * (1.0 / np.sqrt(DIM))
        w_proj = jax.random.normal(k3, (DIM, DIM), dtype=jnp.float32) * (1.0 / np.sqrt(DIM))
        b_proj = jax.random.normal(k4, (DIM,), dtype=jnp.float32) * 0.01
        return {'x': x, 'w_qkv': w_qkv, 'w_proj': w_proj, 'b_proj': b_proj}
    _L0_attn_in = _L0_attn_setup()

    def _L0_ffn_setup():
        import jax, jax.numpy as jnp
        import numpy as np
        B, N, D, E, MULT = (4, 256, 128, 8, 4)
        F = D * MULT

        def _top2_gate(xn, Wg):
            logits = jnp.einsum('bnd,ed->bne', xn, Wg)
            probs = jax.nn.softmax(logits, axis=-1)
            top1 = jnp.argmax(probs, axis=-1)
            t1v = jnp.take_along_axis(probs, top1[..., None], axis=-1)[..., 0]
            masked = jnp.where(jax.nn.one_hot(top1, probs.shape[-1], dtype=bool), -jnp.inf, probs)
            top2 = jnp.argmax(masked, axis=-1)
            t2v = jnp.take_along_axis(masked, top2[..., None], axis=-1)[..., 0]
            denom = t1v + t2v + 1e-09
            combine = jnp.stack([t1v / denom, t2v / denom], axis=-1)
            idx = jnp.stack([top1, top2], axis=-1)
            return (combine, idx)
        key = jax.random.key(seed)
        ks = jax.random.split(key, 8)
        s_in = 1.0 / np.sqrt(D)
        s_hid = 1.0 / np.sqrt(F)
        return {'x': jax.random.normal(ks[0], (B, N, D), dtype=jnp.float32), 'gamma': jnp.ones((D,), dtype=jnp.float32), 'beta': jnp.zeros((D,), dtype=jnp.float32), 'Wg': jax.random.normal(ks[1], (E, D), dtype=jnp.float32) * s_in, 'W1': jax.random.normal(ks[2], (E, D, F), dtype=jnp.float32) * s_in, 'b1': jax.random.normal(ks[3], (E, F), dtype=jnp.float32) * 0.01, 'W2': jax.random.normal(ks[4], (E, F, D), dtype=jnp.float32) * s_hid, 'b2': jax.random.normal(ks[5], (E, D), dtype=jnp.float32) * 0.01}
    _L0_ffn_in = _L0_ffn_setup()
    _L0_c = _w((lambda *s: np.random.randn(*s).astype(np.float32) * 0.05)(8, 128))
    _L0_wmod = _w((lambda *s: np.random.randn(*s).astype(np.float32) * 0.05)(128, 6 * 128) * 128 ** (-0.5))

    def _L1_attn_setup():
        import jax, jax.numpy as jnp
        import numpy as np
        H = 8
        LN_EPS = 1e-05
        key = jax.random.key(seed)
        ks = jax.random.split(key, 4)
        B, S, D = (4, 256, 128)
        x = jax.random.normal(ks[0], (B, S, D), dtype=jnp.float32)
        sc = 1.0 / np.sqrt(D)
        Wq = jax.random.normal(ks[1], (D, D), dtype=jnp.float32) * sc
        Wk = jax.random.normal(ks[2], (D, D), dtype=jnp.float32) * sc
        Wv = jax.random.normal(ks[3], (D, D * H), dtype=jnp.float32) * sc
        return {'x': x, 'Wq': Wq, 'bq': jnp.zeros((D,), jnp.float32), 'Wk': Wk, 'bk': jnp.zeros((D,), jnp.float32), 'Wv': Wv, 'bv': jnp.zeros((D * H,), jnp.float32), 'gamma': jnp.ones((D,), jnp.float32), 'beta': jnp.zeros((D,), jnp.float32)}
    _L1_attn_in = _L1_attn_setup()

    def _L1_ffn_setup():
        import jax, jax.numpy as jnp
        import numpy as np
        B, S, H, E = (2, 1024, 128, 8)
        SCALE = 0.5
        key = jax.random.key(seed)
        k1, k2 = jax.random.split(key)
        x = jax.random.normal(k1, (B, S, H), dtype=jnp.float32)
        gate_w = jax.random.normal(k2, (E, H), dtype=jnp.float32) * 0.02
        coeff = SCALE * (1.0 + 0.05 * jnp.arange(E, dtype=jnp.float32))
        expert_w = coeff[:, None, None] * jnp.eye(H, dtype=jnp.float32)
        return {'x': x, 'gate_w': gate_w, 'expert_w': expert_w}
    _L1_ffn_in = _L1_ffn_setup()
    _L1_c = _w((lambda *s: np.random.randn(*s).astype(np.float32) * 0.05)(8, 128))
    _L1_wmod = _w((lambda *s: np.random.randn(*s).astype(np.float32) * 0.05)(128, 6 * 128) * 128 ** (-0.5))
    _d = {'L0_attn_x': _L0_attn_in['x'], 'L0_attn_w_qkv': _L0_attn_in['w_qkv'], 'L0_attn_w_proj': _L0_attn_in['w_proj'], 'L0_attn_b_proj': _L0_attn_in['b_proj'], 'L0_ffn_gamma': _L0_ffn_in['gamma'], 'L0_ffn_beta': _L0_ffn_in['beta'], 'L0_ffn_Wg': _L0_ffn_in['Wg'], 'L0_ffn_W1': _L0_ffn_in['W1'], 'L0_ffn_b1': _L0_ffn_in['b1'], 'L0_ffn_W2': _L0_ffn_in['W2'], 'L0_ffn_b2': _L0_ffn_in['b2'], 'L0_c': _L0_c, 'L0_wmod': _L0_wmod, 'L1_attn_Wq': _L1_attn_in['Wq'], 'L1_attn_bq': _L1_attn_in['bq'], 'L1_attn_Wk': _L1_attn_in['Wk'], 'L1_attn_bk': _L1_attn_in['bk'], 'L1_attn_Wv': _L1_attn_in['Wv'], 'L1_attn_bv': _L1_attn_in['bv'], 'L1_attn_gamma': _L1_attn_in['gamma'], 'L1_attn_beta': _L1_attn_in['beta'], 'L1_ffn_gate_w': _L1_ffn_in['gate_w'], 'L1_ffn_expert_w': _L1_ffn_in['expert_w'], 'L1_c': _L1_c, 'L1_wmod': _L1_wmod}
    _x0 = _d['L0_attn_x']
    _d['L0_attn_x'] = jax.random.normal(jax.random.fold_in(jax.random.key(seed), 1), (8, 512, 128), dtype=_x0.dtype)
    del _x0
    return _d

def reference(L0_attn_x, L0_attn_w_qkv, L0_attn_w_proj, L0_attn_b_proj, L0_ffn_gamma, L0_ffn_beta, L0_ffn_Wg, L0_ffn_W1, L0_ffn_b1, L0_ffn_W2, L0_ffn_b2, L0_c, L0_wmod, L1_attn_Wq, L1_attn_bq, L1_attn_Wk, L1_attn_bk, L1_attn_Wv, L1_attn_bv, L1_attn_gamma, L1_attn_beta, L1_ffn_gate_w, L1_ffn_expert_w, L1_c, L1_wmod):

    def _L0_attn_ref(x, w_qkv, w_proj, b_proj):
        import jax, jax.numpy as jnp
        import numpy as np
        DIM = 128
        NUM_HEADS = 16
        HEAD_DIM = DIM // NUM_HEADS
        B, N, C = x.shape
        H, D = (NUM_HEADS, C // NUM_HEADS)
        qkv = (x @ w_qkv.T).reshape(B, N, 3, H, D).transpose(2, 0, 3, 1, 4)
        q, k, v = (qkv[0], qkv[1], qkv[2])
        q = jax.nn.elu(q) + 1.0
        k = jax.nn.elu(k) + 1.0
        kv = jnp.einsum('bhnd,bhne->bhde', k, v)
        num = jnp.einsum('bhnd,bhde->bhne', q, kv)
        z = 1.0 / (jnp.einsum('bhnd,bhd->bhn', q, k.sum(axis=2)) + 1e-06)
        out = num * z[..., None]
        out = out.transpose(0, 2, 1, 3).reshape(B, N, C)
        return out @ w_proj.T + b_proj

    def _L0_ffn_ref(x, gamma, beta, Wg, W1, b1, W2, b2):
        import jax, jax.numpy as jnp
        import numpy as np
        B, N, D, E, MULT = (4, 256, 128, 8, 4)
        F = D * MULT

        def _top2_gate(xn, Wg):
            logits = jnp.einsum('bnd,ed->bne', xn, Wg)
            probs = jax.nn.softmax(logits, axis=-1)
            top1 = jnp.argmax(probs, axis=-1)
            t1v = jnp.take_along_axis(probs, top1[..., None], axis=-1)[..., 0]
            masked = jnp.where(jax.nn.one_hot(top1, probs.shape[-1], dtype=bool), -jnp.inf, probs)
            top2 = jnp.argmax(masked, axis=-1)
            t2v = jnp.take_along_axis(masked, top2[..., None], axis=-1)[..., 0]
            denom = t1v + t2v + 1e-09
            combine = jnp.stack([t1v / denom, t2v / denom], axis=-1)
            idx = jnp.stack([top1, top2], axis=-1)
            return (combine, idx)
        residual = x
        mu = jnp.mean(x, axis=-1, keepdims=True)
        var = jnp.mean(jnp.square(x - mu), axis=-1, keepdims=True)
        xn = (x - mu) / jnp.sqrt(var + 1e-05) * gamma + beta
        combine, idx = _top2_gate(xn, Wg)
        n_expert = Wg.shape[0]
        onehot = jax.nn.one_hot(idx, n_expert, dtype=x.dtype)
        gates = jnp.einsum('bns,bnse->ebn', combine, onehot)

        def body(acc, params):
            w1, b1e, w2, b2e, g = params
            h = jax.nn.gelu(jnp.einsum('bnd,df->bnf', xn, w1) + b1e, approximate=True)
            y = jnp.einsum('bnf,fd->bnd', h, w2) + b2e
            return (acc + g[..., None] * y, None)
        out, _ = jax.lax.scan(body, jnp.zeros_like(x), (W1, b1, W2, b2, gates))
        return residual + out

    def _L1_attn_ref(x, Wq, bq, Wk, bk, Wv, bv, gamma, beta):
        import jax, jax.numpy as jnp
        import numpy as np
        H = 8
        LN_EPS = 1e-05
        B, S, D = x.shape
        dk = D // H
        mu = jnp.mean(x, axis=-1, keepdims=True)
        var = jnp.mean(jnp.square(x - mu), axis=-1, keepdims=True)
        xn = (x - mu) * jax.lax.rsqrt(var + LN_EPS) * gamma + beta
        q = (xn @ Wq + bq).reshape(B, S, H, dk).transpose(0, 2, 1, 3)
        k = (xn @ Wk + bk).reshape(B, S, H, dk).transpose(0, 2, 1, 3)
        v = (xn @ Wv + bv).reshape(B, S, H, D).transpose(0, 2, 1, 3)
        scores = jnp.einsum('bhsd,bhtd->bhst', q, k) / jnp.sqrt(jnp.asarray(dk, x.dtype))
        p = jax.nn.softmax(scores, axis=-1)
        att = jnp.einsum('bhst,bhtd->bhsd', p, v)
        out = att.reshape(S, B, D, H).sum(axis=-1).reshape(B, S, D)
        return out

    def _L1_ffn_ref(x, gate_w, expert_w):
        import jax, jax.numpy as jnp
        import numpy as np
        B, S, H, E = (2, 1024, 128, 8)
        SCALE = 0.5
        scores = jnp.einsum('bsh,eh->bse', x, gate_w)
        chosen = jnp.argmax(scores, axis=-1)
        onehot = jax.nn.one_hot(chosen, gate_w.shape[0], dtype=x.dtype)
        expert_out = jnp.einsum('bsh,efh->bsef', x, expert_w)
        return x + jnp.einsum('bsef,bse->bsf', expert_out, onehot)
    x = L0_attn_x
    mod = (_silu(L0_c) @ L0_wmod).reshape(L0_c.shape[0], 6, 1, -1)
    sa, ca, ga, sb, cb, gb = (mod[:, 0], mod[:, 1], mod[:, 2], mod[:, 3], mod[:, 4], mod[:, 5])
    ga = (2 * (ga >= 0) - 1) * jnp.maximum(jnp.abs(ga), 0.25)
    gb = (2 * (gb >= 0) - 1) * jnp.maximum(jnp.abs(gb), 0.25)
    h = _layernorm(x, axis=-1) * (1 + ca) + sa
    x = x + ga * _L0_attn_ref(h, L0_attn_w_qkv, L0_attn_w_proj, L0_attn_b_proj)
    h = _layernorm(x, axis=-1) * (1 + cb) + sb
    x = x + gb * _L0_ffn_ref(h, L0_ffn_gamma, L0_ffn_beta, L0_ffn_Wg, L0_ffn_W1, L0_ffn_b1, L0_ffn_W2, L0_ffn_b2)
    mod = (_silu(L1_c) @ L1_wmod).reshape(L1_c.shape[0], 6, 1, -1)
    sa, ca, ga, sb, cb, gb = (mod[:, 0], mod[:, 1], mod[:, 2], mod[:, 3], mod[:, 4], mod[:, 5])
    ga = (2 * (ga >= 0) - 1) * jnp.maximum(jnp.abs(ga), 0.25)
    gb = (2 * (gb >= 0) - 1) * jnp.maximum(jnp.abs(gb), 0.25)
    h = _layernorm(x, axis=-1) * (1 + ca) + sa
    x = x + ga * _L1_attn_ref(h, L1_attn_Wq, L1_attn_bq, L1_attn_Wk, L1_attn_bk, L1_attn_Wv, L1_attn_bv, L1_attn_gamma, L1_attn_beta)
    h = _layernorm(x, axis=-1) * (1 + cb) + sb
    x = x + gb * _L1_ffn_ref(h, L1_ffn_gate_w, L1_ffn_expert_w)
    return x

_drawn_inputs = setup_inputs


def setup_inputs(seed=0):
    import zlib

    import numpy as np

    out = dict(_drawn_inputs(seed))
    spreads = {'L0_ffn_gamma': (1.0, 0.2),
     'L0_ffn_beta': (0.0, 0.1),
     'L1_attn_bq': (0.0, 0.767),
     'L1_attn_bk': (0.0, 2.0),
     'L1_attn_bv': (0.0, 0.1),
     'L1_attn_gamma': (1.0, 0.2),
     'L1_attn_beta': (0.0, 0.1)}
    factors = {'L0_attn_w_qkv': 3.203,
     'L0_attn_w_proj': 3.242,
     'L0_attn_b_proj': 8.0,
     'L0_ffn_b1': 44.099,
     'L0_ffn_b2': 29.5,
     'L1_ffn_gate_w': 19.97}
    for name, (base, spread) in spreads.items():
        noise = np.random.default_rng([zlib.crc32(name.encode()), seed]).standard_normal(out[name].shape)
        drawn = base * np.exp(spread * noise) if base else spread * noise
        out[name] = jnp.asarray(drawn.astype(out[name].dtype))
    for name, factor in factors.items():
        out[name] = (out[name] * factor).astype(out[name].dtype)
    return out
```

```python
import concourse.bass as bass
from concourse import mybir
from contextlib import ExitStack

f32 = mybir.dt.float32
bf16 = mybir.dt.bfloat16
ALU = mybir.AluOpType
ACT = mybir.ActivationFunctionType
AX = mybir.AxisListType

P = 128
B, S, D = 8, 512, 128
PAIRS = B // 2
NT = 2 * S // P
QL = S // NT
NC = S // P
EPS = 1e-5
E = 8
F = 512
FC = F // P
H0, DH0 = 16, 8
H1, DH1 = 8, 16
KX = DH0 * H0 + H0
NTERM = 6
KS = NTERM * DH1
KM = KS + 3

STEPS = {"A": 11, "B": 29, "C": 48, "D": 56, "PA": 7, "PB": 14, "PC": 14, "PD": 7}


class Own:

    def __init__(self, eng, sem):
        self.eng, self.sem, self.base, self.n, self.i, self.per = eng, sem, 0, 0, None, 0

    def loop(self, i, stage):
        self.base += self.n
        self.i, self.stage, self.per, self.n = i, stage, STEPS[stage], 0

    def end(self, turns):
        assert self.n == self.per, (self.stage, self.n, "steps in a turn, not", self.per)
        self.base, self.i, self.n = self.base + turns * self.per, None, 0

    def count(self, ins):
        ins.then_inc(self.sem, 1)
        self.n += 1

    def wait(self):
        if self.i is None:
            self.eng.wait_ge(self.sem, self.base + self.n)
        else:
            self.eng.wait_ge(self.sem, self.i * self.per + (self.base + self.n))

    def link(self, ins):
        self.count(ins)
        self.wait()


def build(nc, io, out):
    ctx = ExitStack()
    with ctx:
        ctx.enter_context(nc.allow_non_contiguous_dma(reason="small weights, laid out by columns once"))

        def sb(name, shape, dt=f32):
            return ctx.enter_context(nc.sbuf_tensor(name, shape, dt))

        def sem(name):
            return ctx.enter_context(nc.semaphore(name))

        X = sb("X", [P, PAIRS * NT, D])
        modb = sb("modb", [P, 2, PAIRS, 6, D])
        gbias = sb("gbias", [P, PAIRS, D])
        identf = sb("identf", [P, P])
        identb = sb("identb", [P, P], bf16)
        blockmask = sb("blockmask", [P, KX])
        mhalf = sb("mhalf", [P, NT])
        prio = sb("prio", [P, E])
        wqkv_raw = sb("wqkv_raw", [P, 3, D])
        wproj_raw = sb("wproj_raw", [P, D])
        wqkvT = sb("wqkvT", [P, 3, D])
        wprojT = sb("wprojT", [P, D])
        expT = sb("expT", [P, E, D])
        wgT = sb("wgT", [P, E])
        gateT = sb("gateT", [P, E])
        cT = sb("cT", [P, 2, B])
        cs = sb("cs", [P, 2, B])
        cwide = sb("cwide", [P, 2, B, QL])
        W1 = sb("W1", [P, E, F])
        W2 = sb("W2", [P, E, FC, D])
        b1c = sb("b1c", [P, E, FC])
        b2r = sb("b2r", [E, D])
        bproj = sb("bproj", [P, D])
        gam0 = sb("gam0", [P, 1])
        bet0 = sb("bet0", [P, 1])
        gam1 = sb("gam1", [P, 1])
        bet1 = sb("bet1", [P, 1])
        wqkv1 = sb("wqkv1", [P, 3, D])
        bqkv1 = sb("bqkv1", [P, 3, D])
        Hb = sb("Hb", [P, NT, D])
        Zb = sb("Zb", [P, NT, D])
        xT = sb("xT", [P, NT * P])
        st = sb("st", [P, NT, 6])
        mom = sb("mom", [P, NT, 2])
        dm = sb("dm", [P, NT])
        scales = sb("scales", [P, NT, 2])
        half = sb("half", [P, NT])
        epst = sb("epst", [P, NT])
        rstd = sb("rstd", [P, NT])
        A1 = sb("A1", [P, 16384])
        A2 = sb("A2", [P, 6144])

        PS = ctx.enter_context(nc.psum_tensor("PS", [P, 8, 512], f32))
        PSf = PS[:, :, :].rearrange("p b n -> p (b n)")

        def bank(b, n=1):
            return PSf[:, 512 * b:512 * (b + n)]

        own_v, own_p, own_a = sem("own_v"), sem("own_p"), sem("own_a")
        ld = {k: sem("ld_" + k) for k in ("c", "mod", "x", "w0", "wg", "moe", "w1", "v", "bc", "d")}
        consts = sem("consts")
        stats_ready, rstd_ready = sem("stats_ready"), sem("rstd_ready")

        a1 = A1[:, :]
        a2 = A2[:, :]
        wv_raw = a1[:, 0:8 * D].rearrange("p (o j) -> p o j", j=8)
        bv_raw = a1[:, 8 * D:16 * D].rearrange("p (o j) -> p o j", j=8)

        wmod = a1[:, 16 * D:28 * D].rearrange("p (l n) -> p l n", l=2)
        exp_raw = a1[:, 28 * D:36 * D].rearrange("p (e d) -> p e d", e=E)

        block = ctx.enter_context(nc.Block())

        def modrow(blk, pair, j):
            return modb[:, blk, pair, j, :].unsqueeze(1).broadcast_to([P, NT, D])

        def tiles(buf, pair):
            return buf[:, bass.ds(pair * NT, NT), :]

        s_silu, s_mod, s_modc, s_wT, s_wTc, s_wx = (sem(n) for n in (
            "silu_exp", "mod_in_psum", "mod_copied", "weights_transposed", "weights_copied", "weights_in_place"))
        a_h, a_tr, a_hT, a_q, a_kv, a_act, a_phi, a_kvx, a_kvb, a_num, a_o, a_oT, a_oTs, a_pr = (
            sem("a_" + n) for n in ("h", "tr", "hT", "q", "kv", "act", "phi", "kvx", "kvb", "num", "o", "oT", "oTs",
                                    "proj"))
        b_z, b_tr, b_xT, b_lg, b_l, b_e, b_g, b_gT, b_gTs, b_b2, b_mm, b_ge, b_y, b_ac = (
            sem("b_" + n) for n in ("z", "tr", "xT", "logits", "shifted", "exp", "gates", "gT", "gTs",
                                    "b2", "hidden", "gelu", "y", "acc"))
        c_z, c_tr, c_xT, c_qkv, c_sp, c_tk, c_tks, c_tq, c_tqs, c_s1, c_mx, c_mxs, c_tm, c_tms = (
            sem("c_" + n) for n in ("z", "tr", "xT", "qkv", "split", "kT", "kTs", "qT", "qTs", "scores", "max",
                                    "maxsplit", "qmT", "qmTs"))
        c_s2, c_p, c_pv, c_ot, c_fT, c_y, c_x = (
            sem("c_" + n) for n in ("scoresT", "probs", "pv", "out", "outT", "y", "x"))
        d_h, d_tr, d_hT, d_lg, d_mm, d_sel, d_x, d_out = (
            sem("d_" + n) for n in ("h", "tr", "hT", "logits", "expert", "selected", "x", "out"))

        def stats_and_normalise(v, own, src, dst, turn, done=None):
            for t in range(NT):
                last = nc.vector.bn_stats(st[:, t, :], src(t))
            last.then_inc(stats_ready, 1)
            v.wait_ge(rstd_ready, turn)
            for t in range(NT):
                last = nc.vector.tensor_scalar(dst[:, t, :], src(t), mom[:, t, 0:1], rstd[:, t:t + 1],
                                               ALU.subtract, ALU.mult)
            if done is None:
                own.link(last)
            else:
                last.then_inc(done, 1)

        def moments(p, own, turn):
            tt = nc.gpsimd.tensor_tensor
            p.wait_ge(stats_ready, turn)
            own.count(tt(mom[:, :, :], st[:, :, 1:3], st[:, :, 4:6], ALU.add))
            own.link(tt(dm[:, :], st[:, :, 1], st[:, :, 4], ALU.subtract))
            own.count(tt(mom[:, :, :], mom[:, :, :], scales[:, :, :], ALU.mult))
            own.link(tt(dm[:, :], dm[:, :], half[:, :], ALU.mult))
            own.link(tt(dm[:, :], dm[:, :], dm[:, :], ALU.mult))
            own.link(tt(dm[:, :], dm[:, :], mom[:, :, 1], ALU.add))
            own.link(tt(dm[:, :], dm[:, :], epst[:, :], ALU.add))
            tt(rstd[:, :], dm[:, :], mhalf[:, :], ALU.pow).then_inc(rstd_ready, 1)

        NORMS = {"A": 1, "B": 2, "C": 2, "D": 1}
        NB = {"A": 0}
        NB["B"] = NB["A"] + PAIRS * NORMS["A"]
        NB["C"] = NB["B"] + PAIRS * NORMS["B"]
        NB["D"] = NB["C"] + PAIRS * NORMS["C"]

        o = 0

        def take(base, n, off):
            return base[:, off:off + n], off + n
        hq_e, o = take(a1, 2 * S, 0)
        hq_r, o = take(a1, 2 * S, o)
        phiq, o = take(a1, 2 * S, o)
        k_e, o = take(a1, 2 * S, o)
        k_r, o = take(a1, 2 * S, o)
        phik, o = take(a1, 2 * S, o)
        vx, o = take(a1, 2 * NC * 132, o)
        kvb, o = take(a1, 2 * KX, o)
        rden, o = take(a1, 2 * NC * H0, o)
        oa, o = take(a1, 2 * S, o)
        oaT, o = take(a1, 2 * S, o)
        k_e, k_r, phik, oa = (x.rearrange("p (b c d) -> p b c d", b=2, c=NC) for x in (k_e, k_r, phik, oa))
        vx = vx.rearrange("p (b c d) -> p b c d", b=2, c=NC)
        kvb = kvb.rearrange("p (b n) -> p b n", b=2)
        rden = rden.rearrange("p (b c h) -> p b c h", b=2, c=NC)
        xTb = xT[:, :].rearrange("p (b n) -> p b n", b=2)

        hid = a1[:, 0:2 * FC * 512].rearrange("p (r f n) -> p r f n", r=2, f=FC)
        acc = a1[:, 4096:4096 + NT * D].rearrange("p (t d) -> p t d", t=NT)
        gb_ = 4096 + NT * D
        gw = {}
        for k in ("l", "p", "w", "oh1", "oh2", "p2", "g"):
            gw[k] = a1[:, gb_:gb_ + NT * E].rearrange("p (t e) -> p t e", t=NT)
            gb_ += NT * E
        for k in ("m", "s", "t1", "t2", "m1", "den", "rd", "c1", "c2"):
            gw[k] = a1[:, gb_:gb_ + NT]
            gb_ += NT
        gTs = a1[0:E, gb_:gb_ + NT * P]

        probs = a1.rearrange("p (r h c n) -> p r h c n", r=2, h=4, c=NC)

        def over_experts(x):
            return x.unsqueeze(2).broadcast_to([P, NT, E])

        prio_b = prio[:, :].unsqueeze(1).broadcast_to([P, NT, E])

        a2b = a2.bitcast(bf16)
        qst = a2b[:, 0:NC * H1 * 100].rearrange("p (c h k) -> p c h k", c=NC, h=H1)
        kst = a2b[:, 3200:6400].rearrange("p (c h k) -> p c h k", c=NC, h=H1)
        w1f = W1[:, :, :].rearrange("p e f -> p (e f)")
        w2f = W2[:, :, :, :].rearrange("p e c d -> p (e c d)")
        kT = w2f[:, 2048:4096].bitcast(bf16).rearrange("p (h n) -> p h n", h=H1)
        qT = sb("qT", [P, 2, S], bf16)
        qmT = sb("qmT", [P, 2, S], bf16)
        qkv = w1f[:, 0:2048].rearrange("p (b c t d) -> p b c t d", b=2, c=NC, t=2)
        vv = w1f[:, 2048:4096].rearrange("p (b c h k) -> p b c h k", b=2, c=NC, h=H1)
        OT = w2f[:, 0:2048].rearrange("p (g r b q) -> p g r b q", g=2, r=8, b=2)
        mxs = sb("mxs", [P, NC, H1])
        rs1 = sb("rs1", [P, NC * H1 * DH1])
        mr1 = sb("mr1", [P, NC * H1])
        rd1 = sb("rd1", [P, 8, 4])

        def psb(b):
            return bank(b).bitcast(bf16)

        def stage_c_scalar(a):
            with a.Fori(0, PAIRS) as i:
                for j in range(2):
                    a.wait_ge(c_tr, i * 2 + (j + 1))
                    nc.scalar.activation(
                        xT[:, :].rearrange("p (b t q) -> p b t q", b=2, t=NT)[:, :, 4 * j:4 * j + 4, :],
                        bank(j).rearrange("p (t b q) -> p b t q", t=4, b=2), ACT.Identity,
                        bias=bet1[:, :], scale=gam1[:, :]).then_inc(c_xT, 1)
                for bb in range(2):
                    for h in range(H1):
                        n = bb * H1 + h
                        a.wait_ge(c_tk, i * 16 + (n + 1))
                        nc.scalar.copy(kT[0:KM, h, :], psb(0)[0:KM, 0:512]).then_inc(c_tks, 1)
                        a.wait_ge(c_tq, i * 16 + (n + 1))
                        nc.scalar.copy(qT[0:KS, h % 2, :], psb(1)[0:KS, 0:512]).then_inc(c_tqs, 1)
                    for g in range(2):
                        m = bb * 2 + g
                        for hh in range(4):
                            n = bb * H1 + 4 * g + hh
                            a.wait_ge(c_tm, i * 16 + (n + 1))
                            nc.scalar.copy(qmT[0:KM, hh % 2, :], psb(hh % 2)[0:KM, 0:512]).then_inc(c_tms, 1)
                            if hh == 0 and m >= 2:
                                a.wait_ge(c_pv, i * 4 + (m - 1))
                            for c2 in range(2):
                                a.wait_ge(c_s2, i * 32 + (2 * n + c2 + 1))
                                nc.scalar.activation(
                                    probs[:, g, hh, 2 * c2:2 * c2 + 2, :].rearrange("p c n -> p (c n)"),
                                    bank(2 + 2 * c2, 2), ACT.Exp, scale=DH1 ** -0.5).then_inc(c_p, 1)
                        a.wait_ge(c_pv, i * 4 + (m + 1))
                        nc.scalar.copy(OT[:, g, :, bb, :], bank(6).rearrange("p (q r) -> p r q", r=8)).then_inc(c_ot, 1)

        def stack(v, own, dst, src, first, second, third, done=None):
            s4 = src.rearrange("p c (h k) -> p c h k", h=H1)
            r = rs1[:, :].rearrange("p (c h k) -> p c h k", c=NC, h=H1)

            def blk(n):
                return dst[:, :, :, DH1 * n:DH1 * n + DH1]
            s0, n0, t0 = first
            for j in range(n0):
                own.count(nc.vector.tensor_copy(blk(s0 + j * t0), s4))
            own.wait()
            own.link(nc.vector.tensor_tensor(r, s4, blk(s0), ALU.subtract))
            s1, n1, t1 = second
            for j in range(n1):
                own.count(nc.vector.tensor_copy(blk(s1 + j * t1), r))
            own.wait()
            last = nc.vector.tensor_tensor(blk(third), r, blk(s1), ALU.subtract)
            if done is None:
                own.link(last)
            else:
                last.then_inc(done, 1)

        @block.sync
        def _(eng):
            eng.dma_start(cT[:, 0, :], io["L0_c"].rearrange("b d -> d b")).then_inc(ld["c"], 16)
            eng.dma_start(cT[:, 1, :], io["L1_c"].rearrange("b d -> d b")).then_inc(ld["c"], 16)
            eng.dma_start(wmod[:, 0, :], io["L0_wmod"]).then_inc(ld["mod"], 16)
            eng.dma_start(wmod[:, 1, :], io["L1_wmod"]).then_inc(ld["mod"], 16)
            for b in range(B):
                eng.dma_start(X[QL * (b % 2):QL * (b % 2 + 1), NT * (b // 2):NT * (b // 2 + 1), :],
                              io["L0_attn_x"][b].rearrange("(h q) d -> q h d", q=QL)).then_inc(ld["x"], 16)
            for k, t in (("L1_attn_bq", 0), ("L1_attn_bk", 1)):
                eng.dma_start(bqkv1[:, t, :], io[k].unsqueeze(0).broadcast_to([P, D])).then_inc(ld["v"], 16)
            eng.dma_start(a1[:, 8 * D:16 * D], io["L1_attn_bv"].unsqueeze(0).broadcast_to([P, 8 * D]))\
               .then_inc(ld["v"], 16)
            eng.dma_start(a1[:, 0:8 * D], io["L1_attn_Wv"]).then_inc(ld["v"], 16)
            eng.dma_start(W1[:, :, :], io["L0_ffn_W1"].rearrange("e d f -> d e f")).then_inc(ld["moe"], 16)
            eng.dma_start(W2[:, :, :, :], io["L0_ffn_W2"].rearrange("e (c p) d -> p e c d", p=P))\
               .then_inc(ld["moe"], 16)
            eng.dma_start(b2r[:, :], io["L0_ffn_b2"]).then_inc(ld["moe"], 16)
            eng.dma_start(b1c[:, :, :], io["L0_ffn_b1"].rearrange("e (c p) -> p e c", p=P)).then_inc(ld["moe"], 16)
            for pair in range(PAIRS):
                eng.wait_ge(d_x, pair + 1)
                for bb in range(2):
                    eng.dma_start(out[2 * pair + bb].rearrange("(h q) d -> q h d", q=QL),
                                  X[QL * bb:QL * (bb + 1), NT * pair:NT * (pair + 1), :]).then_inc(d_out, 16)
            eng.wait_ge(d_out, 16 * B)

        @block.gpsimd
        def _(p):
            own = Own(p, own_p)
            nc.gpsimd.memset(identf[:, :], 0.0).then_inc(own_p, 1)
            nc.gpsimd.memset(identb[:, :], 0.0).then_inc(own_p, 1)
            nc.gpsimd.memset(blockmask[:, :], 1.0).then_inc(own_p, 1)
            nc.gpsimd.memset(mhalf[:, :], -0.5).then_inc(own_p, 1)
            nc.gpsimd.memset(half[:, :], 0.5).then_inc(own_p, 1)
            nc.gpsimd.memset(epst[:, :], EPS).then_inc(own_p, 1)
            nc.gpsimd.memset(scales[:, :, 0], 0.5).then_inc(own_p, 1)
            nc.gpsimd.memset(scales[:, :, 1], 1.0 / D).then_inc(own_p, 1)
            own.n = 8
            nc.gpsimd.iota(cwide[:, 0, 0, 0:E].bitcast(mybir.dt.int32), [[-1, E]], base=E, channel_multiplier=0)\
                .then_inc(own_p, 1)
            own.n = 9
            own.wait()
            for m in (identf, identb):
                own.count(nc.gpsimd.affine_select(out=m[:, :], in_=m[:, :], compare_op=ALU.not_equal, fill=1.0,
                                                  base=0, pattern=[[-1, P]], channel_multiplier=1))
            own.count(nc.gpsimd.tensor_copy(prio[:, :], cwide[:, 0, 0, 0:E].bitcast(mybir.dt.int32)))
            for c0, cols in ((0, [[-DH0, H0], [0, DH0]]), (D, [[-DH0, H0]])):
                part = blockmask[:, c0:c0 + (D if c0 == 0 else H0)]
                own.wait()
                own.count(nc.gpsimd.affine_select(out=part, in_=part, compare_op=ALU.is_ge, fill=0.0, base=0,
                                                  pattern=cols, channel_multiplier=1))
                own.wait()
                own.count(nc.gpsimd.affine_select(out=part, in_=part, compare_op=ALU.is_ge, fill=0.0, base=DH0 - 1,
                                                  pattern=[[-s, n] for s, n in cols], channel_multiplier=-1))
            own.wait()
            nc.gpsimd.memset(rstd[:, :], 0.0).then_inc(consts, 1)
            p.wait_ge(consts, 1)


            for stage in "ABCD":
                k = NORMS[stage]
                with p.Fori(0, PAIRS) as i:
                    own.loop(i, "P" + stage)
                    for j in range(k):
                        moments(p, own, i * k + (NB[stage] + j + 1))
                own.end(PAIRS)

        @block.scalar
        def _(a):
            a.dma_start(wqkv_raw[:, :, :], io["L0_attn_w_qkv"].rearrange("(t p) d -> p t d", p=P)).then_inc(ld["w0"], 16)
            a.dma_start(wproj_raw[:, :], io["L0_attn_w_proj"]).then_inc(ld["w0"], 16)
            a.dma_start(exp_raw, io["L1_ffn_expert_w"].rearrange("e f h -> f e h")).then_inc(ld["w0"], 16)
            a.dma_start(bproj[:, :], io["L0_attn_b_proj"].unsqueeze(0).broadcast_to([P, D])).then_inc(ld["bc"], 16)
            a.dma_start(wgT[:, :], io["L0_ffn_Wg"].rearrange("e d -> d e")).then_inc(ld["wg"], 16)
            a.dma_start(gateT[:, :], io["L1_ffn_gate_w"].rearrange("e d -> d e")).then_inc(ld["wg"], 16)
            for t, k in ((gam0, "L0_ffn_gamma"), (bet0, "L0_ffn_beta"), (gam1, "L1_attn_gamma"), (bet1, "L1_attn_beta")):
                a.dma_start(t[:, :], io[k].unsqueeze(1)).then_inc(ld["wg"], 16)
            a.dma_start(wqkv1[:, 0, :], io["L1_attn_Wq"]).then_inc(ld["w1"], 16)
            a.dma_start(wqkv1[:, 1, :], io["L1_attn_Wk"]).then_inc(ld["w1"], 16)
            a.wait_ge(ld["c"], 32)
            nc.scalar.activation(cs[:, :, :], cT[:, :, :], ACT.Exp, scale=-1.0).then_inc(s_silu, 1)
            for n in range(2 * PAIRS):
                a.wait_ge(s_mod, n + 1)
                nc.scalar.copy(modb[:, n // PAIRS, n % PAIRS, :, :].rearrange("p j d -> p (j d)"),
                               PSf[:, 1024 * (n % 2):1024 * (n % 2) + 6 * D]).then_inc(s_modc, 1)
            a.wait_ge(s_wT, 1)
            nc.scalar.copy(wqkvT[:, :, :].rearrange("p t d -> p (t d)"), bank(4)[:, 0:3 * D]).then_inc(s_wTc, 1)
            nc.scalar.copy(wprojT[:, :], bank(4)[:, 3 * D:4 * D]).then_inc(s_wTc, 1)
            nc.scalar.copy(expT[:, :, :].rearrange("p e d -> p (e d)"), bank(5, 2)).then_inc(s_wTc, 1)

            with a.Fori(0, PAIRS) as i:
                for j in range(2):
                    a.wait_ge(a_tr, i * 2 + (j + 1))
                    nc.scalar.copy(xT[:, :].rearrange("p (b t q) -> p b t q", b=2, t=NT)[:, :, 4 * j:4 * j + 4, :],
                                   bank(j).rearrange("p (t b q) -> p b t q", t=4, b=2)).then_inc(a_hT, 1)
                for bb in range(2):
                    a.wait_ge(a_q, i * 2 + (bb + 1))
                    sl = slice(S * bb, S * bb + S)
                    nc.scalar.activation(hq_e[:, sl], bank(2 + bb), ACT.Exp)
                    nc.scalar.activation(hq_r[:, sl], bank(2 + bb), ACT.Relu).then_inc(a_act, 1)
                for bb in range(2):
                    a.wait_ge(a_kv, i * 2 + (bb + 1))
                    kv = bank(4 + 2 * bb, 2).rearrange("p (c n) -> p c n", c=NC)
                    nc.scalar.activation(k_e[:, bb], kv[:, :, 0:D], ACT.Exp)
                    nc.scalar.activation(k_r[:, bb], kv[:, :, 0:D], ACT.Relu)
                    nc.scalar.copy(vx[:, bb, :, 0:D], kv[:, :, D:2 * D]).then_inc(a_act, 1)
                for bb in range(2):
                    a.wait_ge(a_oT, i * 2 + (bb + 1))
                    nc.scalar.copy(oaT.rearrange("p (t b q) -> p b t q", b=2, t=NT)[:, bb],
                                   bank(bb).rearrange("p (t q) -> p t q", t=NT)).then_inc(a_oTs, 1)

            with a.Fori(0, PAIRS) as i:
                for j in range(2):
                    a.wait_ge(b_tr, i * 2 + (j + 1))
                    nc.scalar.activation(xT[:, 512 * j:512 * j + 512], bank(j), ACT.Identity,
                                         bias=bet0[:, :], scale=gam0[:, :]).then_inc(b_xT, 1)
                a.wait_ge(b_l, i + 1)
                nc.scalar.activation(gw["p"], gw["l"], ACT.Exp).then_inc(b_e, 1)
                for n in range(2 * E):
                    for fc in range(FC):
                        a.wait_ge(b_mm, i * 64 + (4 * n + fc + 1))
                        if fc == 0 and n >= 2:
                            a.wait_ge(b_y, i * 16 + (n - 1))
                        nc.scalar.activation(hid[:, n % 2, fc, :], bank(4 + fc), ACT.Gelu_apprx_tanh,
                                             bias=b1c[:, n % E, fc:fc + 1]).then_inc(b_ge, 1)

            stage_c_scalar(a)

            with a.Fori(0, PAIRS) as i:
                for j in range(2):
                    a.wait_ge(d_tr, i * 2 + (j + 1))
                    nc.scalar.copy(xT[:, 512 * j:512 * j + 512], bank(j)).then_inc(d_hT, 1)

        @block.vector
        def _(v):
            own = Own(v, own_v)
            v.wait_ge(s_silu, 1)
            own.link(nc.vector.tensor_scalar(cs[:, :, :], cs[:, :, :], 1.0, None, ALU.add))
            own.link(nc.vector.reciprocal(cs[:, :, :], cs[:, :, :]))
            own.link(nc.vector.tensor_tensor(cs[:, :, :], cs[:, :, :], cT[:, :, :], ALU.mult))
            v.wait_ge(consts, 1)
            nc.vector.tensor_copy(cwide[:, :, :, :].rearrange("p l b q -> p (l b) q"),
                                  cs[:, :, :].rearrange("p l b -> p (l b)").unsqueeze(2).broadcast_to([P, 2 * B, QL]))\
                .then_inc(s_wx, 1)
            v.wait_ge(ld["v"], 64)
            own.count(nc.vector.tensor_reduce(wqkv1[:, 2, :], wv_raw, axis=AX.X, op=ALU.add))
            own.link(nc.vector.tensor_reduce(bqkv1[:, 2, :], bv_raw, axis=AX.X, op=ALU.add))
            v.wait_ge(s_modc, 2 * PAIRS)
            for j in (1, 4):
                mj = modb[:, :, :, j, :].rearrange("p l r d -> p (l r) d")
                own.count(nc.vector.tensor_scalar(mj, mj, 1.0, None, ALU.add))
            sgn = Zb[:, :, :]
            mag = Hb[:, :, :]
            for j in (2, 5):
                mj = modb[:, :, :, j, :].rearrange("p l r d -> p (l r) d")
                own.link(nc.vector.tensor_scalar(sgn, mj, 0.0, 2.0, ALU.is_ge, ALU.mult))
                own.link(nc.vector.tensor_scalar(mag, mj, -1.0, None, ALU.mult))
                own.link(nc.vector.tensor_tensor(mag, mag, mj, ALU.max))
                own.link(nc.vector.tensor_scalar(mag, mag, 0.25, None, ALU.max))
                own.link(nc.vector.scalar_tensor_tensor(out=mj, in0=sgn, scalar=-1.0, in1=mag, op0=ALU.add, op1=ALU.mult))
            v.wait_ge(ld["bc"], 16)
            own.link(nc.vector.tensor_tensor(gbias[:, :, :], modb[:, 0, :, 2, :],
                                             bproj[:, :].unsqueeze(1).broadcast_to([P, PAIRS, D]), ALU.mult))
            own.link(nc.vector.memset(vx[:, :, :, D:132], 1.0))

            v.wait_ge(ld["x"], 16 * B)
            with v.Fori(0, PAIRS) as i:
                own.loop(i, "A")
                xt = tiles(X, i)
                stats_and_normalise(v, own, lambda t: X[:, i * NT + t, :], Zb, i + (NB["A"] + 1))
                own.link(nc.vector.tensor_tensor(Zb[:, :, :], Zb[:, :, :], modrow(0, i, 1), ALU.mult))
                nc.vector.tensor_tensor(Hb[:, :, :], Zb[:, :, :], modrow(0, i, 0), ALU.add).then_inc(a_h, 1)
                own.count(nc.vector.tensor_tensor(xt, xt, gbias[:, i, :].unsqueeze(1).broadcast_to([P, NT, D]), ALU.add))
                for bb in range(2):
                    sl = slice(S * bb, S * bb + S)
                    v.wait_ge(a_act, i * 4 + (bb + 1))
                    own.count(nc.vector.scalar_tensor_tensor(out=phiq[:, sl], in0=hq_e[:, sl], scalar=1.0,
                                                             in1=hq_r[:, sl], op0=ALU.min, op1=ALU.add))
                for bb in range(2):
                    v.wait_ge(a_act, i * 4 + (bb + 3))
                    nc.vector.scalar_tensor_tensor(out=phik[:, bb], in0=k_e[:, bb], scalar=1.0,
                                                   in1=k_r[:, bb], op0=ALU.min, op1=ALU.add).then_inc(a_phi, 1)
                for bb in range(2):
                    v.wait_ge(a_kvx, i * 2 + (bb + 1))
                    nc.vector.tensor_tensor(kvb[:, bb, 0:D], bank(bb)[:, 0:D], blockmask[:, 0:D], ALU.mult)
                    nc.vector.tensor_scalar(kvb[:, bb, D:KX], blockmask[:, D:KX], bank(bb)[:, D:D + 1], None,
                                            ALU.mult).then_inc(a_kvb, 1)
                for bb in range(2):
                    v.wait_ge(a_num, i * 2 + (bb + 1))
                    num = bank(4 + 2 * bb, 2).rearrange("p (c n) -> p c n", c=NC)
                    own.link(nc.vector.tensor_scalar(rden[:, bb], num[:, :, D:KX], 1e-6, None, ALU.add))
                    own.link(nc.vector.reciprocal(rden[:, bb], rden[:, bb]))
                    for c in range(NC):
                        last = nc.vector.tensor_tensor(
                            oa[:, bb, c].rearrange("p (h e) -> p h e", h=H0),
                            num[:, c, 0:D].rearrange("p (h e) -> p h e", h=H0),
                            rden[:, bb, c].unsqueeze(2).broadcast_to([P, H0, DH0]), ALU.mult)
                    last.then_inc(a_o, 1)
                v.wait_ge(a_pr, i + 1)
                own.link(nc.vector.tensor_tensor(Zb[:, :, :], bank(2, 2).rearrange("p (t d) -> p t d", t=NT),
                                                 modrow(0, i, 2), ALU.mult))
                own.link(nc.vector.tensor_tensor(xt, xt, Zb[:, :, :], ALU.add))
            own.end(PAIRS)

            with v.Fori(0, PAIRS) as i:
                own.loop(i, "B")
                xt = tiles(X, i)
                stats_and_normalise(v, own, lambda t: X[:, i * NT + t, :], Zb, i * 2 + (NB["B"] + 1))
                own.link(nc.vector.tensor_tensor(Zb[:, :, :], Zb[:, :, :], modrow(0, i, 4), ALU.mult))
                own.link(nc.vector.tensor_tensor(Hb[:, :, :], Zb[:, :, :], modrow(0, i, 3), ALU.add))
                own.link(nc.vector.tensor_tensor(Zb[:, :, :], Hb[:, :, :], modrow(0, i, 5), ALU.mult))
                own.link(nc.vector.tensor_tensor(xt, xt, Zb[:, :, :], ALU.add))
                stats_and_normalise(v, own, lambda t: Hb[:, t, :], Zb, i * 2 + (NB["B"] + 2), b_z)
                g = gw
                v.wait_ge(b_lg, i + 1)
                lg = bank(2)[:, 0:NT * E].rearrange("p (t e) -> p t e", t=NT)
                own.link(nc.vector.tensor_reduce(g["m"], lg, axis=AX.X, op=ALU.max))
                nc.vector.tensor_tensor(g["l"], lg, over_experts(g["m"]), ALU.subtract).then_inc(b_l, 1)
                v.wait_ge(b_e, i + 1)
                own.link(nc.vector.tensor_reduce(g["s"], g["p"], axis=AX.X, op=ALU.add))
                own.link(nc.vector.reciprocal(g["s"], g["s"]))
                own.link(nc.vector.tensor_tensor(g["p"], g["p"], over_experts(g["s"]), ALU.mult))

                def first_of_largest(p, t, oh):
                    own.link(nc.vector.tensor_reduce(g[t], g[p], axis=AX.X, op=ALU.max))
                    own.link(nc.vector.tensor_tensor(g["w"], g[p], over_experts(g[t]), ALU.is_ge))
                    own.link(nc.vector.tensor_tensor(g["w"], g["w"], prio_b, ALU.mult))
                    own.link(nc.vector.tensor_reduce(g["m1"], g["w"], axis=AX.X, op=ALU.max))
                    own.link(nc.vector.tensor_tensor(g[oh], g["w"], over_experts(g["m1"]), ALU.is_equal))
                first_of_largest("p", "t1", "oh1")
                own.link(nc.vector.scalar_tensor_tensor(out=g["p2"], in0=g["oh1"], scalar=-4.0, in1=g["p"],
                                                        op0=ALU.mult, op1=ALU.add))
                first_of_largest("p2", "t2", "oh2")
                own.link(nc.vector.scalar_tensor_tensor(out=g["den"], in0=g["t1"], scalar=1e-9, in1=g["t2"],
                                                        op0=ALU.add, op1=ALU.add))
                own.link(nc.vector.reciprocal(g["rd"], g["den"]))
                own.count(nc.vector.tensor_tensor(g["c1"], g["t1"], g["rd"], ALU.mult))
                own.link(nc.vector.tensor_tensor(g["c2"], g["t2"], g["rd"], ALU.mult))
                own.count(nc.vector.tensor_tensor(g["oh1"], g["oh1"], over_experts(g["c1"]), ALU.mult))
                own.link(nc.vector.tensor_tensor(g["oh2"], g["oh2"], over_experts(g["c2"]), ALU.mult))
                nc.vector.tensor_tensor(g["g"], g["oh1"], g["oh2"], ALU.add).then_inc(b_g, 1)
                v.wait_ge(b_gT, i + 1)
                nc.vector.tensor_copy(gTs, bank(2, 2)[0:E, :]).then_inc(b_gTs, 1)
                v.wait_ge(b_b2, i + 1)
                own.link(nc.vector.tensor_copy(acc, bank(0, 2).rearrange("p (t d) -> p t d", t=NT)))
                for n in range(2 * E):
                    v.wait_ge(b_y, i * 16 + (n + 1))
                    for t in range(4):
                        tt = 4 * (n // E) + t
                        last = nc.vector.scalar_tensor_tensor(
                            out=acc[:, tt, :], in0=bank(2 + n % 2)[:, D * t:D * t + D],
                            scalar=g["g"][:, tt, n % E:n % E + 1], in1=acc[:, tt, :], op0=ALU.mult, op1=ALU.add)
                    last.then_inc(b_ac, 1)
                    v.wait_ge(b_ac, i * 16 + (n + 1))
                own.link(nc.vector.tensor_tensor(acc, acc, modrow(0, i, 5), ALU.mult))
                own.link(nc.vector.tensor_tensor(xt, xt, acc, ALU.add))
            own.end(PAIRS)

            for bb in range(2):
                own.count(nc.vector.memset(vv[:, bb, :, :, DH1:DH1 + 1], 1.0))
                own.count(nc.vector.memset(vv[:, bb, :, :, DH1 + 1:32], 0.0))
            own.link(nc.vector.memset(kst[:, :, :, KS:100], -1.0))
            with v.Fori(0, PAIRS) as i:
                own.loop(i, "C")
                xt = tiles(X, i)
                stats_and_normalise(v, own, lambda t: X[:, i * NT + t, :], Zb, i * 2 + (NB["C"] + 1))
                own.link(nc.vector.tensor_tensor(Zb[:, :, :], Zb[:, :, :], modrow(1, i, 1), ALU.mult))
                own.link(nc.vector.tensor_tensor(Hb[:, :, :], Zb[:, :, :], modrow(1, i, 0), ALU.add))
                stats_and_normalise(v, own, lambda t: Hb[:, t, :], Zb, i * 2 + (NB["C"] + 2), c_z)
                for bb in range(2):
                    for c in range(NC):
                        v.wait_ge(c_qkv, i * 8 + (bb * NC + c + 1))
                        b = bank(2 + c)
                        nc.vector.tensor_tensor(qkv[:, bb, c], b[:, 0:2 * D].rearrange("p (t d) -> p t d", t=2),
                                                bqkv1[:, 0:2, :], ALU.add)
                        own.count(nc.vector.tensor_tensor(
                            vv[:, bb, c, :, 0:DH1], b[:, 2 * D:3 * D].rearrange("p (h d) -> p h d", h=H1),
                            bqkv1[:, 2, :].rearrange("p (h d) -> p h d", h=H1), ALU.add))
                    own.wait()
                    stack(v, own, qst, qkv[:, bb, :, 0, :], (0, 3, 1), (3, 2, 2), 4)
                    stack(v, own, kst, qkv[:, bb, :, 1, :], (2, 3, 1), (1, 2, 4), 0, c_sp)
                    for h in range(H1):
                        for c in range(NC):
                            n = (bb * H1 + h) * NC + c
                            v.wait_ge(c_s1, i * 64 + (n + 1))
                            nc.vector.tensor_reduce(mxs[:, c, h:h + 1], bank(2 + n % 4), axis=AX.X, op=ALU.max)\
                                .then_inc(c_mx, 1)
                    v.wait_ge(c_mx, i * 64 + 32 * (bb + 1))
                    mq = qst[:, :, :, KS:KM]
                    mr = mr1[:, :].rearrange("p (c h) -> p c h", c=NC)
                    own.link(nc.vector.tensor_copy(mq[:, :, :, 0], mxs[:, :, :]))
                    own.link(nc.vector.tensor_tensor(mr, mxs[:, :, :], mq[:, :, :, 0], ALU.subtract))
                    own.link(nc.vector.tensor_copy(mq[:, :, :, 1], mr))
                    nc.vector.tensor_tensor(mq[:, :, :, 2], mr, mq[:, :, :, 1], ALU.subtract).then_inc(c_mxs, 1)
                    v.wait_ge(c_mxs, i * 2 + (bb + 1))
                for g in range(2):
                    v.wait_ge(c_fT, i * 2 + (g + 1))
                    t = bank(2 + 2 * g, 2).rearrange("p (r h k) -> p r h k", r=8, h=4)
                    own.link(nc.vector.reciprocal(rd1[:, :, :], t[:, :, :, DH1]))
                    for hh in range(4):
                        last = nc.vector.tensor_tensor(
                            Zb[:, 4 * g + hh, :].rearrange("p (r k) -> p r k", r=8), t[:, :, hh, 0:DH1],
                            rd1[:, :, hh].unsqueeze(2).broadcast_to([P, 8, DH1]), ALU.mult)
                    own.link(last)
                own.link(nc.vector.tensor_tensor(Zb[:, :, :], Zb[:, :, :], modrow(1, i, 2), ALU.mult))
                nc.vector.tensor_tensor(xt, xt, Zb[:, :, :], ALU.add).then_inc(c_x, 1)
                v.wait_ge(c_x, i + 1)
            own.end(PAIRS)

            with v.Fori(0, PAIRS) as i:
                own.loop(i, "D")
                xt = tiles(X, i)
                g = gw
                stats_and_normalise(v, own, lambda t: X[:, i * NT + t, :], Zb, i + (NB["D"] + 1))
                own.link(nc.vector.tensor_tensor(Zb[:, :, :], Zb[:, :, :], modrow(1, i, 4), ALU.mult))
                nc.vector.tensor_tensor(Hb[:, :, :], Zb[:, :, :], modrow(1, i, 3), ALU.add).then_inc(d_h, 1)
                v.wait_ge(d_h, i + 1)
                v.wait_ge(d_lg, i + 1)
                lg = bank(2)[:, 0:NT * E].rearrange("p (t e) -> p t e", t=NT)
                own.link(nc.vector.tensor_reduce(g["m"], lg, axis=AX.X, op=ALU.max))
                own.link(nc.vector.tensor_tensor(g["w"], lg, over_experts(g["m"]), ALU.is_ge))
                own.link(nc.vector.tensor_tensor(g["w"], g["w"], prio_b, ALU.mult))
                own.link(nc.vector.tensor_reduce(g["m1"], g["w"], axis=AX.X, op=ALU.max))
                own.link(nc.vector.tensor_tensor(g["oh1"], g["w"], over_experts(g["m1"]), ALU.is_equal))
                for t in range(NT):
                    for e2 in range(2):
                        n = 2 * t + e2
                        v.wait_ge(d_mm, i * 16 + (n + 1))
                        for e in range(4 * e2, 4 * e2 + 4):
                            pick = nc.vector.scalar_tensor_tensor(
                                out=Hb[:, t, :], in0=bank(4 + n % 4)[:, D * (e % 4):D * (e % 4) + D],
                                scalar=g["oh1"][:, t, e:e + 1], in1=Hb[:, t, :], op0=ALU.mult, op1=ALU.add)
                            if e % 4 < 3:
                                own.link(pick)
                        pick.then_inc(d_sel, 1)
                        v.wait_ge(d_sel, i * 16 + (n + 1))
                own.link(nc.vector.tensor_tensor(Hb[:, :, :], Hb[:, :, :], modrow(1, i, 5), ALU.mult))
                nc.vector.tensor_tensor(xt, xt, Hb[:, :, :], ALU.add).then_inc(d_x, 1)
            own.end(PAIRS)

        @block.tensor
        def _(pe):
            pe.wait_ge(consts, 1)
            pe.wait_ge(ld["w0"], 48)
            for t in range(3):
                nc.tensor.transpose(bank(4)[:, D * t:D * t + D], wqkv_raw[:, t, :], identf[:, :])
            nc.tensor.transpose(bank(4)[:, 3 * D:4 * D], wproj_raw[:, :], identf[:, :])
            for e in range(E):
                last = nc.tensor.transpose(bank(5, 2)[:, D * e:D * e + D], exp_raw[:, e, :], identf[:, :])
            last.then_inc(s_wT, 1)
            pe.wait_ge(s_wx, 1)
            pe.wait_ge(ld["mod"], 32)
            for n in range(2 * PAIRS):
                if n >= 2:
                    pe.wait_ge(s_modc, n - 1)
                l, r = n // PAIRS, n % PAIRS
                lhs = cwide[:, l, 2 * r:2 * r + 2, :].rearrange("p b q -> p (b q)")
                b = 2 * (n % 2)
                nc.tensor.matmul(bank(b), lhs, wmod[:, l, 0:512], start=True, stop=True)
                nc.tensor.matmul(bank(b + 1)[:, 0:256], lhs, wmod[:, l, 512:768], start=True, stop=True)\
                    .then_inc(s_mod, 1)
            pe.wait_ge(s_wTc, 3)
            pe.wait_ge(s_modc, 2 * PAIRS)

            def transpose_tiles(src, done):
                for t in range(NT):
                    last = nc.tensor.transpose(bank(t // 4)[:, P * (t % 4):P * (t % 4) + P], src[:, t, :], identf[:, :])
                    if t % 4 == 3:
                        last.then_inc(done, 1)

            with pe.Fori(0, PAIRS) as i:
                pe.wait_ge(a_h, i + 1)
                transpose_tiles(Hb, a_tr)
                pe.wait_ge(a_hT, i * 2 + 2)
                for bb in range(2):
                    nc.tensor.matmul(bank(2 + bb), wqkvT[:, 0, :], xTb[:, bb, :], start=True, stop=True)\
                        .then_inc(a_q, 1)
                for bb in range(2):
                    for c in range(NC):
                        last = nc.tensor.matmul(bank(4 + 2 * bb, 2)[:, 256 * c:256 * c + 256],
                                                xTb[:, bb, P * c:P * c + P],
                                                wqkvT[:, 1:3, :].rearrange("p t d -> p (t d)"), start=True, stop=True)
                    last.then_inc(a_kv, 1)
                for bb in range(2):
                    pe.wait_ge(a_phi, i * 2 + (bb + 1))
                    for c in range(NC):
                        last = nc.tensor.matmul(bank(bb)[:, 0:D + 1], phik[:, bb, c, :], vx[:, bb, c, 0:D + 1],
                                                start=(c == 0), stop=(c == NC - 1))
                    last.then_inc(a_kvx, 1)
                for bb in range(2):
                    pe.wait_ge(a_kvb, i * 2 + (bb + 1))
                    for c in range(NC):
                        last = nc.tensor.matmul(bank(4 + 2 * bb, 2)[:, 256 * c:256 * c + KX],
                                                phiq[:, S * bb + P * c:S * bb + P * c + P], kvb[:, bb, :],
                                                start=True, stop=True)
                    last.then_inc(a_num, 1)
                for bb in range(2):
                    pe.wait_ge(a_o, i * 2 + (bb + 1))
                    for c in range(NC):
                        last = nc.tensor.transpose(bank(bb)[:, P * c:P * c + P], oa[:, bb, c, :], identf[:, :])
                    last.then_inc(a_oT, 1)
                pe.wait_ge(a_oTs, i * 2 + 2)
                for t in range(NT):
                    last = nc.tensor.matmul(bank(2 + t // 4)[:, D * (t % 4):D * (t % 4) + D], oaT[:, P * t:P * t + P], wprojT[:, :],
                                            start=True, stop=True)
                last.then_inc(a_pr, 1)

            pe.wait_ge(ld["wg"], 96)
            pe.wait_ge(ld["moe"], 64)
            with pe.Fori(0, PAIRS) as i:
                pe.wait_ge(b_z, i + 1)
                transpose_tiles(Zb, b_tr)
                pe.wait_ge(b_xT, i * 2 + 2)
                for t in range(NT):
                    last = nc.tensor.matmul(bank(2)[:, E * t:E * t + E], xT[:, P * t:P * t + P], wgT[:, :],
                                            start=True, stop=True)
                last.then_inc(b_lg, 1)
                pe.wait_ge(b_g, i + 1)
                for t in range(NT):
                    last = nc.tensor.transpose(bank(2, 2)[0:E, P * t:P * t + P], gw["g"][:, t, :], identf[:, :])
                last.then_inc(b_gT, 1)
                pe.wait_ge(b_gTs, i + 1)
                for t in range(NT):
                    last = nc.tensor.matmul(bank(0, 2)[:, D * t:D * t + D], gTs[:, P * t:P * t + P], b2r[:, :],
                                            start=True, stop=True)
                last.then_inc(b_b2, 1)

                def hidden(n):
                    for fc in range(FC):
                        if n:
                            pe.wait_ge(b_ge, i * 64 + (4 * (n - 1) + fc + 1))
                        nc.tensor.matmul(bank(4 + fc), W1[:, n % E, P * fc:P * fc + P],
                                         xT[:, 512 * (n // E):512 * (n // E) + 512], start=True, stop=True)\
                            .then_inc(b_mm, 1)

                def second(n):
                    pe.wait_ge(b_ge, i * 64 + 4 * (n + 1))
                    if n >= 2:
                        pe.wait_ge(b_ac, i * 16 + (n - 1))
                    for t in range(4):
                        for fc in range(FC):
                            last = nc.tensor.matmul(bank(2 + n % 2)[:, D * t:D * t + D],
                                                    hid[:, n % 2, fc, P * t:P * t + P], W2[:, n % E, fc, :],
                                                    start=(fc == 0), stop=(fc == FC - 1))
                    last.then_inc(b_y, 1)
                for n in range(2 * E):
                    hidden(n)
                    if n:
                        second(n - 1)
                second(2 * E - 1)

            pe.wait_ge(ld["w1"], 32)
            with pe.Fori(0, PAIRS) as i:
                pe.wait_ge(c_z, i + 1)
                transpose_tiles(Zb, c_tr)
                pe.wait_ge(c_xT, i * 2 + 2)
                for bb in range(2):
                    for c in range(NC):
                        if bb == 1 and c == 0:
                            pe.wait_ge(c_p, i * 32 + 16)
                        nc.tensor.matmul(bank(2 + c)[:, 0:3 * D], xTb[:, bb, P * c:P * c + P],
                                         wqkv1[:, :, :].rearrange("p t d -> p (t d)"), start=True, stop=True)\
                            .then_inc(c_qkv, 1)
                    pe.wait_ge(c_sp, i * 2 + (bb + 1))
                    for h in range(H1):
                        n = bb * H1 + h
                        for c in range(NC):
                            last = nc.tensor.transpose(psb(0)[0:KM, P * c:P * c + P], kst[:, c, h, 0:KM], identb[:, :])
                        last.then_inc(c_tk, 1)
                        for c in range(NC):
                            last = nc.tensor.transpose(psb(1)[0:KS, P * c:P * c + P], qst[:, c, h, 0:KS], identb[:, :])
                        last.then_inc(c_tq, 1)
                        pe.wait_ge(c_tks, i * 16 + (n + 1))
                        pe.wait_ge(c_tqs, i * 16 + (n + 1))
                        for c in range(NC):
                            k = n * NC + c
                            if k >= 4:
                                pe.wait_ge(c_mx, i * 64 + (k - 3))
                            nc.tensor.matmul(bank(2 + k % 4), qT[0:KS, h % 2, P * c:P * c + P], kT[0:KS, h, :],
                                             start=True, stop=True).then_inc(c_s1, 1)
                    pe.wait_ge(c_mxs, i * 2 + (bb + 1))
                    for g in range(2):
                        m = bb * 2 + g
                        for hh in range(4):
                            h = 4 * g + hh
                            n = bb * H1 + h
                            if hh >= 2:
                                pe.wait_ge(c_tms, i * 16 + (n - 1))
                            for c in range(NC):
                                last = nc.tensor.transpose(psb(hh % 2)[0:KM, P * c:P * c + P], qst[:, c, h, 0:KM],
                                                           identb[:, :])
                            last.then_inc(c_tm, 1)
                            pe.wait_ge(c_tms, i * 16 + (n + 1))
                            for c in range(NC):
                                if c % 2 == 0 and 2 * n + c // 2 >= 2:
                                    pe.wait_ge(c_p, i * 32 + (2 * n + c // 2 - 1))
                                last = nc.tensor.matmul(bank(2 + c), kT[0:KM, h, P * c:P * c + P],
                                                        qmT[0:KM, hh % 2, :], start=True, stop=True)
                                if c % 2:
                                    last.then_inc(c_s2, 1)
                        pe.wait_ge(c_p, i * 32 + 8 * (m + 1))
                        if m:
                            pe.wait_ge(c_ot, i * 4 + m)
                        for c in range(NC):
                            for hh in range(4):
                                last = nc.tensor.matmul(bank(6)[32 * hh:32 * hh + 32, :], vv[:, bb, c, 4 * g + hh, :],
                                                        probs[:, g, hh, c, :], start=(c == 0), stop=(c == NC - 1))
                        last.then_inc(c_pv, 1)
                pe.wait_ge(c_ot, i * 4 + 4)
                for g in range(2):
                    for r in range(8):
                        src = OT[:, g, r].rearrange("p b q -> p (b q)")
                        last = nc.tensor.transpose(bank(2 + 2 * g, 2)[:, P * r:P * r + P], src, identf[:, :])
                    last.then_inc(c_fT, 1)
                pe.wait_ge(c_x, i + 1)

            with pe.Fori(0, PAIRS) as i:
                pe.wait_ge(d_h, i + 1)
                transpose_tiles(Hb, d_tr)
                pe.wait_ge(d_hT, i * 2 + 2)
                for t in range(NT):
                    last = nc.tensor.matmul(bank(2)[:, E * t:E * t + E], xT[:, P * t:P * t + P], gateT[:, :],
                                            start=True, stop=True)
                last.then_inc(d_lg, 1)
                for t in range(NT):
                    for e2 in range(2):
                        n = 2 * t + e2
                        if n >= 4:
                            pe.wait_ge(d_sel, i * 16 + (n - 3))
                        nc.tensor.matmul(bank(4 + n % 4), xT[:, P * t:P * t + P],
                                         expT[:, 4 * e2:4 * e2 + 4, :].rearrange("p e d -> p (e d)"),
                                         start=True, stop=True).then_inc(d_mm, 1)



_INS = ['L0_attn_x', 'L0_attn_w_qkv', 'L0_attn_w_proj', 'L0_attn_b_proj', 'L0_ffn_gamma', 'L0_ffn_beta', 'L0_ffn_Wg',
        'L0_ffn_W1', 'L0_ffn_b1', 'L0_ffn_W2', 'L0_ffn_b2', 'L0_c', 'L0_wmod', 'L1_attn_Wq', 'L1_attn_bq', 'L1_attn_Wk',
        'L1_attn_bk', 'L1_attn_Wv', 'L1_attn_bv', 'L1_attn_gamma', 'L1_attn_beta', 'L1_ffn_gate_w', 'L1_ffn_expert_w',
        'L1_c', 'L1_wmod']


def kernel(**inputs):
    import numpy as _np
    import concourse.bacc as _bacc
    from concourse import mybir as _mybir
    from concourse.bass_utils import run_bass_kernel_spmd as _run

    nc = _bacc.Bacc("TRN2", target_bir_lowering=False, num_devices=1)
    arrays, io = {}, {}
    for name in _INS:
        a = _np.ascontiguousarray(inputs[name])
        arrays[f"in_{name}_dram"] = a
        io[name] = nc.dram_tensor(f"in_{name}_dram", a.shape, _mybir.dt.from_np(a.dtype), kind="ExternalInput").ap()
    out = nc.dram_tensor("out_0_dram", (B, S, D), _mybir.dt.float32, kind="ExternalOutput").ap()
    build(nc, io, out)
    r = _run(nc, [arrays], core_ids=[0])
    return r.results[0]["out_0_dram"]
```

```python
import concourse.bass as bass
from concourse import mybir
from contextlib import ExitStack

f32 = mybir.dt.float32
bf16 = mybir.dt.bfloat16
ALU = mybir.AluOpType
ACT = mybir.ActivationFunctionType
AX = mybir.AxisListType

P = 128
B, S, D = 8, 512, 128
PAIRS = B // 2
NT = 2 * S // P
QL = S // NT
NC = S // P
EPS = 1e-5
E = 8
F = 512
FC = F // P
H0, DH0 = 16, 8
H1, DH1 = 8, 16
KX = DH0 * H0 + H0
NTERM = 6
KS = NTERM * DH1
KM = KS + 3

STEPS = {"D": 72, "PA": 7, "PB": 14, "PD": 7}


class Own:

    def __init__(self, eng, sem):
        self.eng, self.sem, self.base, self.n, self.i, self.per = eng, sem, 0, 0, None, 0

    def loop(self, i, stage):
        self.base += self.n
        self.i, self.stage, self.per, self.n = i, stage, STEPS[stage], 0

    def end(self, turns):
        assert self.n == self.per, (self.stage, self.n, "steps in a turn, not", self.per)
        self.base, self.i, self.n = self.base + turns * self.per, None, 0

    def count(self, ins):
        ins.then_inc(self.sem, 1)
        self.n += 1

    def wait(self, back=0):
        if self.i is None:
            self.eng.wait_ge(self.sem, self.base + self.n - back)
        else:
            self.eng.wait_ge(self.sem, self.i * self.per + (self.base + self.n - back))

    def link(self, ins):
        self.count(ins)
        self.wait()


def build(nc, io, out):
    ctx = ExitStack()
    with ctx:
        ctx.enter_context(nc.allow_non_contiguous_dma(reason="small weights, laid out by columns once"))

        def sb(name, shape, dt=f32):
            return ctx.enter_context(nc.sbuf_tensor(name, shape, dt))

        def sem(name):
            return ctx.enter_context(nc.semaphore(name))

        X = sb("X", [P, PAIRS * NT, D])
        modb = sb("modb", [P, 2, PAIRS, 6, D])
        gbias = sb("gbias", [P, PAIRS, D])
        identf = sb("identf", [P, P])
        identb = sb("identb", [P, P], bf16)
        blockmask = sb("blockmask", [P, KX])
        mhalf = sb("mhalf", [P, NT])
        prio = sb("prio", [P, E])
        wqkv_raw = sb("wqkv_raw", [P, 3, D])
        wproj_raw = sb("wproj_raw", [P, D])
        wqkvT = sb("wqkvT", [P, 3, D])
        wprojT = sb("wprojT", [P, D])
        expT = sb("expT", [P, E, D])
        wgT = sb("wgT", [P, E])
        gateT = sb("gateT", [P, E])
        cT = sb("cT", [P, 2, B])
        cs = sb("cs", [P, 2, B])
        W1 = sb("W1", [P, E, F])
        W2 = sb("W2", [P, E, FC, D])
        b1c = sb("b1c", [P, E, FC])
        b2r = sb("b2r", [E, D])
        bproj = sb("bproj", [P, D])
        gam0 = sb("gam0", [P, 1])
        bet0 = sb("bet0", [P, 1])
        gam1 = sb("gam1", [P, 1])
        bet1 = sb("bet1", [P, 1])
        wqkv1 = sb("wqkv1", [P, 3, D])
        bqkv1 = sb("bqkv1", [P, 3, D])
        Hb = sb("Hb", [P, NT, D])
        Zb = sb("Zb", [P, NT, D])
        xT = sb("xT", [P, NT * P])
        st = sb("st", [P, NT, 6])
        mom = sb("mom", [P, NT, 2])
        dm = sb("dm", [P, NT])
        scales = sb("scales", [P, NT, 2])
        half = sb("half", [P, NT])
        epst = sb("epst", [P, NT])
        rstd = sb("rstd", [P, NT])
        A1 = sb("A1", [P, 16384])
        A2 = sb("A2", [P, 6144])

        PS = ctx.enter_context(nc.psum_tensor("PS", [P, 8, 512], f32))
        PSf = PS[:, :, :].rearrange("p b n -> p (b n)")

        def bank(b, n=1):
            return PSf[:, 512 * b:512 * (b + n)]

        own_v, own_p, own_a = sem("own_v"), sem("own_p"), sem("own_a")
        ld = {k: sem("ld_" + k) for k in ("c", "mod", "x", "w0", "wg", "moe", "w1", "v", "bc", "d")}
        consts = sem("consts")
        stats_ready, rstd_ready = sem("stats_ready"), sem("rstd_ready")

        a1 = A1[:, :]
        a2 = A2[:, :]
        wv_raw = a1[:, 0:8 * D].rearrange("p (o j) -> p o j", j=8)
        bv_raw = a1[:, 8 * D:16 * D].rearrange("p (o j) -> p o j", j=8)

        wmod = a1[:, 16 * D:28 * D].rearrange("p (l n) -> p l n", l=2)
        exp_raw = a1[:, 28 * D:36 * D].rearrange("p (e d) -> p e d", e=E)
        cwide = a1[:, 44 * D:52 * D].rearrange("p (l b q) -> p l b q", l=2, b=B)

        block = ctx.enter_context(nc.Block())

        def modrow(blk, pair, j):
            return modb[:, blk, pair, j, :].unsqueeze(1).broadcast_to([P, NT, D])

        def tiles(buf, pair):
            return buf[:, bass.ds(pair * NT, NT), :]

        s_silu, s_mod, s_modc, s_wT, s_wTc, s_wx = (sem(n) for n in (
            "silu_exp", "mod_in_psum", "mod_copied", "weights_transposed", "weights_copied", "weights_in_place"))
        a_h, a_tr, a_hT, a_q, a_kv, a_act, a_phi, a_kvx, a_kvb, a_num, a_o, a_oT, a_oTs, a_pr, a_ga = (
            sem("a_" + n) for n in ("h", "tr", "hT", "q", "kv", "act", "phi", "kvx", "kvb", "num", "o", "oT", "oTs",
                                    "proj", "gated"))
        b_z, b_tr, b_xT, b_lg, b_l, b_e, b_g, b_gT, b_gTs, b_b2, b_mm, b_ge, b_y, b_ac, b_ac0 = (
            sem("b_" + n) for n in ("z", "tr", "xT", "logits", "shifted", "exp", "gates", "gT", "gTs",
                                    "b2", "hidden", "gelu", "y", "acc", "acc_begun"))
        c_ready, c_z, c_tr, c_qkv, c_sp, c_spk, c_tk, c_s1, c_mxs, c_tm, c_s2, c_p, c_pv, c_ot, c_fT, c_fr, c_b0, c_b1, c_b6 = (
            sem("c_" + n) for n in ("ready", "z", "tr", "qkv", "split", "ksplit", "kqT", "scores", "maxsplit", "qmT", "scoresT",
                                    "probs", "pv", "out", "outT", "outT_read", "bank0_read", "bank1_read",
                                    "bank67_read"))
        d_h, d_tr, d_hT, d_lg, d_mm, d_sel, d_x, d_out = (
            sem("d_" + n) for n in ("h", "tr", "hT", "logits", "expert", "selected", "x", "out"))

        def stats_and_normalise(v, own, src, dst, turn, done=None):
            for t in range(NT):
                last = nc.vector.bn_stats(st[:, t, :], src(t))
            last.then_inc(stats_ready, 1)
            v.wait_ge(rstd_ready, turn)
            for t in range(NT):
                last = nc.vector.tensor_scalar(dst[:, t, :], src(t), mom[:, t, 0:1], rstd[:, t:t + 1],
                                               ALU.subtract, ALU.mult)
            if done is None:
                own.link(last)
            else:
                last.then_inc(done, 1)

        def moments(p, own, turn):
            tt = nc.gpsimd.tensor_tensor
            p.wait_ge(stats_ready, turn)
            own.count(tt(mom[:, :, :], st[:, :, 1:3], st[:, :, 4:6], ALU.add))
            own.link(tt(dm[:, :], st[:, :, 1], st[:, :, 4], ALU.subtract))
            own.count(tt(mom[:, :, :], mom[:, :, :], scales[:, :, :], ALU.mult))
            own.link(tt(dm[:, :], dm[:, :], half[:, :], ALU.mult))
            own.link(tt(dm[:, :], dm[:, :], dm[:, :], ALU.mult))
            own.link(tt(dm[:, :], dm[:, :], mom[:, :, 1], ALU.add))
            own.link(tt(dm[:, :], dm[:, :], epst[:, :], ALU.add))
            tt(rstd[:, :], dm[:, :], mhalf[:, :], ALU.pow).then_inc(rstd_ready, 1)

        NORMS = {"A": 1, "B": 2, "C": 2, "D": 1}
        NB = {"A": 0}
        NB["B"] = NB["A"] + PAIRS * NORMS["A"]
        NB["C"] = NB["B"] + PAIRS * NORMS["B"]
        NB["D"] = NB["C"] + PAIRS * NORMS["C"]

        o = 0

        def take(base, n, off):
            return base[:, off:off + n], off + n
        hq_e, o = take(a1, 2 * S, 0)
        hq_r, o = take(a1, 2 * S, o)
        phiq, o = take(a1, 2 * S, o)
        k_e, o = take(a1, 2 * S, o)
        k_r, o = take(a1, 2 * S, o)
        phik, o = take(a1, 2 * S, o)
        vx, o = take(a1, 2 * NC * 132, o)
        kvb, o = take(a1, 2 * KX, o)
        rden, o = take(a1, 2 * NC * H0, o)
        oa, o = take(a1, 2 * S, o)
        oaT, o = take(a1, 2 * S, o)
        k_e, k_r, phik, oa = (x.rearrange("p (b c d) -> p b c d", b=2, c=NC) for x in (k_e, k_r, phik, oa))
        vx = vx.rearrange("p (b c d) -> p b c d", b=2, c=NC)
        kvb = kvb.rearrange("p (b n) -> p b n", b=2)
        rden = rden.rearrange("p (b c h) -> p b c h", b=2, c=NC)
        xTb = xT[:, :].rearrange("p (b n) -> p b n", b=2)

        hid = a1[:, 0:2 * FC * 512].rearrange("p (r f n) -> p r f n", r=2, f=FC)
        acc = a1[:, 4096:4096 + NT * D].rearrange("p (t d) -> p t d", t=NT)
        gb_ = 4096 + NT * D
        gw = {}
        for k in ("l", "p", "w", "oh1", "oh2", "p2", "g"):
            gw[k] = a1[:, gb_:gb_ + NT * E].rearrange("p (t e) -> p t e", t=NT)
            gb_ += NT * E
        for k in ("m", "s", "t1", "t2", "m1", "den", "rd", "c1", "c2"):
            gw[k] = a1[:, gb_:gb_ + NT]
            gb_ += NT
        gates = [gw["g"], a1[:, 13312:13312 + NT * E].rearrange("p (t e) -> p t e", t=NT)]
        xTs = [xT[:, :], a1[:, 12288:12288 + NT * P]]
        gTs = a1[0:E, gb_:gb_ + NT * P]

        probs = a1.rearrange("p (r h c n) -> p r h c n", r=2, h=4, c=NC)

        def over_experts(x):
            return x.unsqueeze(2).broadcast_to([P, NT, E])

        prio_b = prio[:, :].unsqueeze(1).broadcast_to([P, NT, E])

        w1f = W1[:, :, :].rearrange("p e f -> p (e f)")
        w2f = W2[:, :, :, :].rearrange("p e c d -> p (e c d)")
        m0f = modb[:, 0].rearrange("p r j d -> p (r j d)")
        STK = NC * H1 * 100

        def stacked(x):
            return x.rearrange("p (c h k) -> p c h k", c=NC, h=H1)
        stk2 = sb("stk2", [P, 2, STK], bf16)
        qst = [stacked(a2.bitcast(bf16)[:, STK * k:STK * (k + 1)]) for k in range(3)]
        kst = [stacked(stk2[:, k, :]) for k in range(2)]
        kT = [x.bitcast(bf16).rearrange("p (h n) -> p h n", h=H1) for x in (w2f[:, 2048:4096], m0f[:, 0:2048])]
        kqT = m0f[:, 2048:2560].bitcast(bf16).rearrange("p (r n) -> p r n", r=2)
        qmT = m0f[:, 2560:3072].bitcast(bf16).rearrange("p (r n) -> p r n", r=2)
        qkv = w1f[:, 0:1024].rearrange("p (c t d) -> p c t d", c=NC, t=2)
        vv = w1f[:, 1024:4096].rearrange("p (b c h k) -> p b c h k", b=3, c=NC, h=H1)
        OT = w2f[:, 0:2048].rearrange("p (g r b q) -> p g r b q", g=2, r=8, b=2)
        mxs = sb("mxs", [P, NC, H1])
        rs1 = sb("rs1", [P, NC * H1 * DH1])
        mr1 = sb("mr1", [P, NC * H1])
        rs2 = sb("rs2", [P, NC * H1 * DH1])
        dm2 = sb("dm2", [P, 1])
        rd1 = sb("rd1", [P, 8, 4])

        def psb(b):
            return bank(b).bitcast(bf16)

        ITEMS = [("pro", 0, 0), ("qkv", 0, 0), ("t1", 0, 0)]
        LAG, HEADS = 10, B * H1

        def head(kind, k):
            if 0 <= k < HEADS:
                ITEMS.append((kind, k // H1, k % H1))
        for k in range(HEADS + LAG + 2):
            slot, h = k // H1, k % H1
            head("t1", k + 1)
            head("t2", k + 1 - LAG)
            head("s1", k)
            head("s2", k - LAG)
            if (k - LAG - 1) % 4 == 3 and k > LAG:
                head("pv", k - LAG - 1)
            if (k - LAG - 2) % (2 * H1) == 2 * H1 - 1 and k >= LAG + 2:
                ITEMS.append(("fin", (k - LAG - 2) // (2 * H1), 0))
            if slot < B - 1 and h == 3:
                ITEMS.append(("qkv", slot + 1, 0))
            if slot % 2 == 0 and slot < B - 2 and h == 4:
                ITEMS.append(("pro", slot // 2 + 1, 0))
        ITEMS = [(kind, b, h // 4 if kind == "pv" else h) for kind, b, h in ITEMS]

        def schedule():
            seen = {}
            for kind, b, h in ITEMS:
                yield kind, b, h, dict(seen)
                seen[kind] = seen.get(kind, 0) + 1

        def uses(n):
            g = n.get
            return (g("pro", 0) + g("t1", 0), g("pro", 0) + g("t2", 0),
                    4 * g("qkv", 0) + 4 * g("s1", 0) + 2 * g("fin", 0),
                    4 * g("s2", 0) + 2 * g("fin", 0))

        def stage_c_scalar(a):
            for kind, b, h, n in schedule():
                u0, u1, u6, u2 = uses(n)
                if kind == "pro":
                    for j in range(2):
                        a.wait_ge(c_tr, 2 * b + j + 1)
                        if j == 0 and b:
                            a.wait_ge(c_qkv, 8 * b * NC // 4)
                        nc.scalar.activation(
                            xT[:, :].rearrange("p (b t q) -> p b t q", b=2, t=NT)[:, :, 4 * j:4 * j + 4, :],
                            bank(j).rearrange("p (t b q) -> p b t q", t=4, b=2), ACT.Identity,
                            bias=bet1[:, :], scale=gam1[:, :]).then_inc((c_b0, c_b1)[j], 1)
                if kind == "t1":
                    t1 = n.get("t1", 0)
                    a.wait_ge(c_tk, t1 + 1)
                    nc.scalar.copy(kT[b % 2][0:KM, h, :], psb(0)[0:KM, 0:512])
                    if t1 >= 2:
                        a.wait_ge(c_s1, 4 * (t1 - 1))
                    nc.scalar.copy(kqT[0:KS, h % 2, :], psb(0)[0:KS, 512:1024]).then_inc(c_b0, 1)
                if kind == "t2":
                    t2 = n.get("t2", 0)
                    a.wait_ge(c_tm, t2 + 1)
                    if t2 >= 2:
                        a.wait_ge(c_s2, 4 * (t2 - 1))
                    nc.scalar.copy(qmT[0:KM, h % 2, :], psb(1)[0:KM, 0:512]).then_inc(c_b1, 1)
                if kind == "s2":
                    r2 = n.get("s2", 0)
                    g = h // 4
                    if h % 4 == 0 and 2 * b + g >= 2:
                        a.wait_ge(c_pv, 2 * b + g - 1)
                    for c in range(NC):
                        a.wait_ge(c_s2, 4 * r2 + c + 1)
                        nc.scalar.activation(probs[:, g, h % 4, c, :], bank(2 + (4 * r2 + c) % 3), ACT.Exp,
                                             scale=DH1 ** -0.5).then_inc(c_p, 1)
                if kind == "pv":
                    a.wait_ge(c_pv, 2 * b + h + 1)
                    if b % 2 == 0 and b and h == 0:
                        a.wait_ge(c_fT, b)
                    nc.scalar.copy(OT[:, h, :, b % 2, :], bank(5).rearrange("p (q r) -> p r q", r=8)).then_inc(c_ot, 1)

        def stage_c_vector(v, own):
            for bb in range(3):
                own.count(nc.vector.memset(vv[:, bb, :, :, DH1:DH1 + 1], 1.0))
                own.count(nc.vector.memset(vv[:, bb, :, :, DH1 + 1:32], 0.0))
            own.link(nc.vector.memset(stk2[:, :, :], -1.0))
            nc.vector.memset(mxs[:, :, :], 0.0).then_inc(c_ready, 1)
            v.wait_ge(c_ready, 1)
            norm = NB["C"]
            for kind, b, h, n in schedule():
                u0, u1, u6, u2 = uses(n)
                if kind == "pro":
                    xt = tiles(X, b)
                    if b:
                        v.wait_ge(c_tr, 2 * b)
                    stats_and_normalise(v, own, lambda t: X[:, b * NT + t, :], Zb, norm + 1)
                    own.link(nc.vector.tensor_tensor(Zb[:, :, :], Zb[:, :, :], modrow(1, b, 1), ALU.mult))
                    own.link(nc.vector.tensor_tensor(Hb[:, :, :], Zb[:, :, :], modrow(1, b, 0), ALU.add))
                    stats_and_normalise(v, own, lambda t: Hb[:, t, :], Zb, norm + 2, c_z)
                    norm += 2
                if kind == "qkv":
                    if b >= 3:
                        v.wait_ge(c_pv, 2 * (b - 2))
                    if b:
                        v.wait_ge(c_sp, b)
                    for c in range(NC):
                        v.wait_ge(c_qkv, NC * b + c + 1)
                        ps = bank(6 + (u6 + c) % 2)
                        nc.vector.tensor_tensor(qkv[:, c], ps[:, 0:2 * D].rearrange("p (t d) -> p t d", t=2),
                                                bqkv1[:, 0:2, :], ALU.add)
                        nc.vector.tensor_tensor(
                            vv[:, b % 3, c, :, 0:DH1], ps[:, 2 * D:3 * D].rearrange("p (h d) -> p h d", h=H1),
                            bqkv1[:, 2, :].rearrange("p (h d) -> p h d", h=H1), ALU.add).then_inc(c_b6, 1)
                    v.wait_ge(c_b6, u6 + 4 - 2 * n.get("fin", 0))
                    if b >= 2:
                        v.wait_ge(c_tk, H1 * (b - 1))
                    stack(nc.vector, own, kst[b % 2], qkv[:, :, 1, :], (2, 3, 1), (1, 2, 4), 0, rs2, c_spk)
                    v.wait_ge(c_spk, b + 1)
                if kind == "s1":
                    for c in range(NC):
                        v.wait_ge(c_s1, 4 * n.get("s1", 0) + c + 1)
                        nc.vector.tensor_reduce(mxs[:, c, h:h + 1], bank(6 + (u6 + c) % 2), axis=AX.X, op=ALU.max)\
                            .then_inc(c_b6, 1)
                    if h == H1 - 1:
                        v.wait_ge(c_b6, u6 + 4 - 2 * n.get("fin", 0))
                        mq = qst[b % 3][:, :, :, KS:KM]
                        mr = mr1[:, :].rearrange("p (c h) -> p c h", c=NC)
                        own.link(nc.vector.tensor_copy(mq[:, :, :, 0], mxs[:, :, :]))
                        own.link(nc.vector.tensor_tensor(mr, mxs[:, :, :], mq[:, :, :, 0], ALU.subtract))
                        own.link(nc.vector.tensor_copy(mq[:, :, :, 1], mr))
                        nc.vector.tensor_tensor(mq[:, :, :, 2], mr, mq[:, :, :, 1], ALU.subtract).then_inc(c_mxs, 1)
                        v.wait_ge(c_mxs, b + 1)
                if kind == "fin":
                    xt = tiles(X, b)
                    v.wait_ge(c_tr, 2 * min(b + 2, PAIRS))
                    for g in range(2):
                        v.wait_ge(c_fT, 2 * b + g + 1)
                        ps = bank(6, 2) if g == 0 else bank(2, 2)
                        t = ps.rearrange("p (r h k) -> p r h k", r=8, h=4)
                        own.link(nc.vector.reciprocal(rd1[:, :, :], t[:, :, :, DH1]))
                        for hh in range(4):
                            last = nc.vector.tensor_tensor(
                                Zb[:, 4 * g + hh, :].rearrange("p (r k) -> p r k", r=8), t[:, :, hh, 0:DH1],
                                rd1[:, :, hh].unsqueeze(2).broadcast_to([P, 8, DH1]), ALU.mult)
                        last.then_inc(c_fr, 1)
                        v.wait_ge(c_fr, 2 * b + g + 1)
                    own.link(nc.vector.tensor_tensor(Zb[:, :, :], Zb[:, :, :], modrow(1, b, 2), ALU.mult))
                    own.link(nc.vector.tensor_tensor(xt, xt, Zb[:, :, :], ALU.add))

        def stage_c_gpsimd(p, own):
            p.wait_ge(c_ready, 1)
            turn = NB["C"]
            for kind, b, h, n in schedule():
                if kind == "pro":
                    moments(p, own, turn + 1)
                    moments(p, own, turn + 2)
                    turn += 2
                if kind == "qkv":
                    p.wait_ge(c_b6, uses(n)[2] + 4 - 2 * n.get("fin", 0))
                    if b >= 3:
                        p.wait_ge(c_tm, H1 * (b - 2))
                    stack(nc.gpsimd, own, qst[b % 3], qkv[:, :, 0, :], (0, 3, 1), (3, 2, 2), 4, rs1, c_sp)

        def done_by(b, h, kind):
            at = ITEMS.index((kind, b, h))
            return sum(k in ("pro", kind) for k, _, _ in ITEMS[:at + 1])

        def stage_c_tensor(pe):
            beside = None
            for at, (kind, b, h, n) in enumerate(schedule()):
                u0, u1, u6, u2 = uses(n)
                fins = n.get("fin", 0)
                if kind == "pro":
                    pe.wait_ge(c_z, b + 1)
                    if u0:
                        pe.wait_ge(c_b0, u0)
                        pe.wait_ge(c_b1, u1)
                    transpose_tiles(pe, Zb, c_tr)
                if kind == "qkv":
                    if b % 2 == 0:
                        pe.wait_ge(c_b0, u0)
                        pe.wait_ge(c_b1, u1)
                    for c in range(NC):
                        if u6 + c >= 2:
                            pe.wait_ge(c_b6, u6 + c - 1 - 2 * fins)
                        if fins and c < 2:
                            pe.wait_ge(c_fr, 2 * fins)
                        nc.tensor.matmul(bank(6 + (u6 + c) % 2)[:, 0:3 * D], xTb[:, b % 2, P * c:P * c + P],
                                         wqkv1[:, :, :].rearrange("p t d -> p (t d)"), start=True, stop=True)\
                            .then_inc(c_qkv, 1)
                if kind == "t1":
                    if h == 0:
                        pe.wait_ge(c_sp, b + 1)
                        pe.wait_ge(c_spk, b + 1)
                    pe.wait_ge(c_b0, u0)
                    for c in range(NC):
                        nc.tensor.transpose(psb(0)[0:KM, P * c:P * c + P], kst[b % 2][:, c, h, 0:KM], identb[:, :])
                    for c in range(NC):
                        last = nc.tensor.transpose(psb(0)[0:KS, 512 + P * c:512 + P * c + P],
                                                   qst[b % 3][:, c, h, 0:KS], identb[:, :])
                    last.then_inc(c_tk, 1)
                if kind == "t2":
                    if h == 0:
                        pe.wait_ge(c_mxs, b + 1)
                    pe.wait_ge(c_b1, u1)
                    for c in range(NC):
                        last = nc.tensor.transpose(psb(1)[0:KM, P * c:P * c + P], qst[b % 3][:, c, h, 0:KM],
                                                   identb[:, :])
                    last.then_inc(c_tm, 1)
                if kind == "s1":
                    def round1(c, b=b, h=h, u6=u6, fins=fins):
                        if c == 0:
                            pe.wait_ge(c_b0, done_by(b, h, "t1"))
                        pe.wait_ge(c_b6, u6 + c - 1 - 2 * fins)
                        if fins and c < 2:
                            pe.wait_ge(c_fr, 2 * fins)
                        nc.tensor.matmul(bank(6 + (u6 + c) % 2), kqT[0:KS, h % 2, P * c:P * c + P],
                                         kT[b % 2][0:KS, h, :], start=True, stop=True).then_inc(c_s1, 1)
                    if at + 1 < len(ITEMS) and ITEMS[at + 1][0] == "s2":
                        beside = round1
                    else:
                        for c in range(NC):
                            round1(c)
                if kind == "s2":
                    r2 = n.get("s2", 0)
                    for c in range(NC):
                        if beside is not None:
                            beside(c)
                        if c == 0:
                            pe.wait_ge(c_b1, done_by(b, h, "t2"))
                        k = 4 * r2 + c
                        if k >= 3:
                            pe.wait_ge(c_p, k - 2)
                        if fins and c < 3:
                            pe.wait_ge(c_fr, 2 * fins)
                        nc.tensor.matmul(bank(2 + k % 3), kT[b % 2][0:KM, h, P * c:P * c + P], qmT[0:KM, h % 2, :],
                                         start=True, stop=True).then_inc(c_s2, 1)
                    beside = None
                if kind == "pv":
                    pe.wait_ge(c_p, 32 * b + 16 * (h + 1))
                    if b or h:
                        pe.wait_ge(c_ot, 2 * b + h)
                    for c in range(NC):
                        for hh in range(4):
                            last = nc.tensor.matmul(bank(5)[32 * hh:32 * hh + 32, :], vv[:, b % 3, c, 4 * h + hh, :],
                                                    probs[:, h, hh, c, :], start=(c == 0), stop=(c == NC - 1))
                    last.then_inc(c_pv, 1)
                if kind == "fin":
                    pe.wait_ge(c_ot, 4 * (b + 1))
                    pe.wait_ge(c_b6, u6 - 2 * fins)
                    pe.wait_ge(c_p, 4 * n["s2"])
                    for g in range(2):
                        for r in range(8):
                            src = OT[:, g, r].rearrange("p b q -> p (b q)")
                            last = nc.tensor.transpose((bank(6, 2) if g == 0 else bank(2, 2))[:, P * r:P * r + P], src,
                                                       identf[:, :])
                        last.then_inc(c_fT, 1)

        def transpose_tiles(pe, src, done):
            for t in range(NT):
                last = nc.tensor.transpose(bank(t // 4)[:, P * (t % 4):P * (t % 4) + P], src[:, t, :], identf[:, :])
                if t % 4 == 3:
                    last.then_inc(done, 1)

        def stack(eng, own, dst, src, first, second, third, rest, done):
            s4 = src.rearrange("p c (h k) -> p c h k", h=H1)
            r = rest[:, :].rearrange("p (c h k) -> p c h k", c=NC, h=H1)

            def blk(n):
                return dst[:, :, :, DH1 * n:DH1 * n + DH1]
            s0, n0, t0 = first
            for j in range(n0):
                own.count(eng.tensor_copy(blk(s0 + j * t0), s4))
            own.wait()
            own.link(eng.tensor_tensor(r, s4, blk(s0), ALU.subtract))
            s1, n1, t1 = second
            for j in range(n1):
                own.count(eng.tensor_copy(blk(s1 + j * t1), r))
            own.wait()
            last = eng.tensor_tensor(blk(third), r, blk(s1), ALU.subtract)
            last.then_inc(done, 1)

        @block.sync
        def _(eng):
            eng.dma_start(cT[:, 0, :], io["L0_c"].rearrange("b d -> d b")).then_inc(ld["c"], 16)
            eng.dma_start(cT[:, 1, :], io["L1_c"].rearrange("b d -> d b")).then_inc(ld["c"], 16)
            eng.dma_start(wmod[:, 0, :], io["L0_wmod"]).then_inc(ld["mod"], 16)
            eng.dma_start(wmod[:, 1, :], io["L1_wmod"]).then_inc(ld["mod"], 16)
            for b in range(B):
                eng.dma_start(X[QL * (b % 2):QL * (b % 2 + 1), NT * (b // 2):NT * (b // 2 + 1), :],
                              io["L0_attn_x"][b].rearrange("(h q) d -> q h d", q=QL)).then_inc(ld["x"], 16)
            for k, t in (("L1_attn_bq", 0), ("L1_attn_bk", 1)):
                eng.dma_start(bqkv1[:, t, :], io[k].unsqueeze(0).broadcast_to([P, D])).then_inc(ld["v"], 16)
            eng.dma_start(a1[:, 8 * D:16 * D], io["L1_attn_bv"].unsqueeze(0).broadcast_to([P, 8 * D]))\
               .then_inc(ld["v"], 16)
            eng.dma_start(a1[:, 0:8 * D], io["L1_attn_Wv"]).then_inc(ld["v"], 16)
            eng.dma_start(W1[:, :, :], io["L0_ffn_W1"].rearrange("e d f -> d e f")).then_inc(ld["moe"], 16)
            eng.dma_start(W2[:, :, :, :], io["L0_ffn_W2"].rearrange("e (c p) d -> p e c d", p=P))\
               .then_inc(ld["moe"], 16)
            eng.dma_start(b2r[:, :], io["L0_ffn_b2"]).then_inc(ld["moe"], 16)
            eng.dma_start(b1c[:, :, :], io["L0_ffn_b1"].rearrange("e (c p) -> p e c", p=P)).then_inc(ld["moe"], 16)
            for pair in range(PAIRS):
                eng.wait_ge(d_x, pair + 1)
                for bb in range(2):
                    eng.dma_start(out[2 * pair + bb].rearrange("(h q) d -> q h d", q=QL),
                                  X[QL * bb:QL * (bb + 1), NT * pair:NT * (pair + 1), :]).then_inc(d_out, 16)
            eng.wait_ge(d_out, 16 * B)

        @block.gpsimd
        def _(p):
            own = Own(p, own_p)
            nc.gpsimd.memset(identf[:, :], 0.0).then_inc(own_p, 1)
            nc.gpsimd.memset(identb[:, :], 0.0).then_inc(own_p, 1)
            nc.gpsimd.memset(blockmask[:, :], 1.0).then_inc(own_p, 1)
            nc.gpsimd.memset(mhalf[:, :], -0.5).then_inc(own_p, 1)
            nc.gpsimd.memset(half[:, :], 0.5).then_inc(own_p, 1)
            nc.gpsimd.memset(epst[:, :], EPS).then_inc(own_p, 1)
            nc.gpsimd.memset(scales[:, :, 0], 0.5).then_inc(own_p, 1)
            nc.gpsimd.memset(scales[:, :, 1], 1.0 / D).then_inc(own_p, 1)
            own.n = 8
            nc.gpsimd.iota(cwide[:, 0, 0, 0:E].bitcast(mybir.dt.int32), [[-1, E]], base=E, channel_multiplier=0)\
                .then_inc(own_p, 1)
            own.n = 9
            own.wait()
            for m in (identf, identb):
                own.count(nc.gpsimd.affine_select(out=m[:, :], in_=m[:, :], compare_op=ALU.not_equal, fill=1.0,
                                                  base=0, pattern=[[-1, P]], channel_multiplier=1))
            own.count(nc.gpsimd.tensor_copy(prio[:, :], cwide[:, 0, 0, 0:E].bitcast(mybir.dt.int32)))
            for c0, cols in ((0, [[-DH0, H0], [0, DH0]]), (D, [[-DH0, H0]])):
                part = blockmask[:, c0:c0 + (D if c0 == 0 else H0)]
                own.wait()
                own.count(nc.gpsimd.affine_select(out=part, in_=part, compare_op=ALU.is_ge, fill=0.0, base=0,
                                                  pattern=cols, channel_multiplier=1))
                own.wait()
                own.count(nc.gpsimd.affine_select(out=part, in_=part, compare_op=ALU.is_ge, fill=0.0, base=DH0 - 1,
                                                  pattern=[[-s, n] for s, n in cols], channel_multiplier=-1))
            own.wait()
            nc.gpsimd.memset(rstd[:, :], 0.0).then_inc(consts, 1)
            p.wait_ge(consts, 1)


            for stage in "ABCD":
                k = NORMS[stage]
                if stage == "C":
                    stage_c_gpsimd(p, own)
                    continue
                with p.Fori(0, PAIRS) as i:
                    own.loop(i, "P" + stage)
                    for j in range(k):
                        moments(p, own, i * k + (NB[stage] + j + 1))
                own.end(PAIRS)

        @block.scalar
        def _(a):
            a.dma_start(wqkv_raw[:, :, :], io["L0_attn_w_qkv"].rearrange("(t p) d -> p t d", p=P)).then_inc(ld["w0"], 16)
            a.dma_start(wproj_raw[:, :], io["L0_attn_w_proj"]).then_inc(ld["w0"], 16)
            a.dma_start(exp_raw, io["L1_ffn_expert_w"].rearrange("e f h -> f e h")).then_inc(ld["w0"], 16)
            a.dma_start(bproj[:, :], io["L0_attn_b_proj"].unsqueeze(0).broadcast_to([P, D])).then_inc(ld["bc"], 16)
            a.dma_start(wgT[:, :], io["L0_ffn_Wg"].rearrange("e d -> d e")).then_inc(ld["wg"], 16)
            a.dma_start(gateT[:, :], io["L1_ffn_gate_w"].rearrange("e d -> d e")).then_inc(ld["wg"], 16)
            for t, k in ((gam0, "L0_ffn_gamma"), (bet0, "L0_ffn_beta"), (gam1, "L1_attn_gamma"), (bet1, "L1_attn_beta")):
                a.dma_start(t[:, :], io[k].unsqueeze(1)).then_inc(ld["wg"], 16)
            a.dma_start(wqkv1[:, 0, :], io["L1_attn_Wq"]).then_inc(ld["w1"], 16)
            a.dma_start(wqkv1[:, 1, :], io["L1_attn_Wk"]).then_inc(ld["w1"], 16)
            a.wait_ge(ld["c"], 32)
            nc.scalar.activation(cs[:, :, :], cT[:, :, :], ACT.Exp, scale=-1.0).then_inc(s_silu, 1)
            for n in range(2 * PAIRS):
                a.wait_ge(s_mod, n + 1)
                nc.scalar.copy(modb[:, n // PAIRS, n % PAIRS, :, :].rearrange("p j d -> p (j d)"),
                               PSf[:, 1024 * (n % 2):1024 * (n % 2) + 6 * D]).then_inc(s_modc, 1)
            a.wait_ge(s_wT, 1)
            nc.scalar.copy(wqkvT[:, :, :].rearrange("p t d -> p (t d)"), bank(4)[:, 0:3 * D]).then_inc(s_wTc, 1)
            nc.scalar.copy(wprojT[:, :], bank(4)[:, 3 * D:4 * D]).then_inc(s_wTc, 1)
            nc.scalar.copy(expT[:, :, :].rearrange("p e d -> p (e d)"), bank(5, 2)).then_inc(s_wTc, 1)

            with a.Fori(0, PAIRS) as i:
                for j in range(2):
                    a.wait_ge(a_tr, i * 2 + (j + 1))
                    nc.scalar.copy(xT[:, :].rearrange("p (b t q) -> p b t q", b=2, t=NT)[:, :, 4 * j:4 * j + 4, :],
                                   bank(j).rearrange("p (t b q) -> p b t q", t=4, b=2)).then_inc(a_hT, 1)
                for bb in range(2):
                    a.wait_ge(a_q, i * 2 + (bb + 1))
                    sl = slice(S * bb, S * bb + S)
                    nc.scalar.activation(hq_e[:, sl], bank(2 + bb), ACT.Exp)
                    nc.scalar.activation(hq_r[:, sl], bank(2 + bb), ACT.Relu).then_inc(a_act, 1)
                for bb in range(2):
                    a.wait_ge(a_kv, i * 2 + (bb + 1))
                    kv = bank(4 + 2 * bb, 2).rearrange("p (c n) -> p c n", c=NC)
                    nc.scalar.activation(k_e[:, bb], kv[:, :, 0:D], ACT.Exp)
                    nc.scalar.activation(k_r[:, bb], kv[:, :, 0:D], ACT.Relu)
                    nc.scalar.copy(vx[:, bb, :, 0:D], kv[:, :, D:2 * D]).then_inc(a_act, 1)
                for bb in range(2):
                    a.wait_ge(a_oT, i * 2 + (bb + 1))
                    nc.scalar.copy(oaT.rearrange("p (t b q) -> p b t q", b=2, t=NT)[:, bb],
                                   bank(bb).rearrange("p (t q) -> p t q", t=NT)).then_inc(a_oTs, 1)

            def scale_b(i):
                for j in range(2):
                    a.wait_ge(b_tr, i * 2 + (j + 1))
                    nc.scalar.activation(xTs[i % 2][:, 512 * j:512 * j + 512], bank(j), ACT.Identity,
                                         bias=bet0[:, :], scale=gam0[:, :]).then_inc(b_xT, 1)

            def exp_b(i):
                a.wait_ge(b_l, i + 1)
                nc.scalar.activation(gw["p"], gw["l"], ACT.Exp).then_inc(b_e, 1)

            scale_b(0)
            exp_b(0)
            for i in range(PAIRS):
                for n in range(2 * E):
                    if i + 1 < PAIRS and n == 8:
                        scale_b(i + 1)
                    if i + 1 < PAIRS and n == 12:
                        exp_b(i + 1)
                    for fc in range(FC):
                        a.wait_ge(b_mm, i * 64 + (4 * n + fc + 1))
                        if fc == 0 and n >= 2:
                            a.wait_ge(b_y, i * 16 + (n - 1))
                        nc.scalar.activation(hid[:, n % 2, fc, :], bank(4 + fc), ACT.Gelu_apprx_tanh,
                                             bias=b1c[:, n % E, fc:fc + 1]).then_inc(b_ge, 1)

            stage_c_scalar(a)

            with a.Fori(0, PAIRS) as i:
                for j in range(2):
                    a.wait_ge(d_tr, i * 2 + (j + 1))
                    nc.scalar.copy(xT[:, 512 * j:512 * j + 512], bank(j)).then_inc(d_hT, 1)

        @block.vector
        def _(v):
            own = Own(v, own_v)
            v.wait_ge(s_silu, 1)
            own.link(nc.vector.tensor_scalar(cs[:, :, :], cs[:, :, :], 1.0, None, ALU.add))
            own.link(nc.vector.reciprocal(cs[:, :, :], cs[:, :, :]))
            own.link(nc.vector.tensor_tensor(cs[:, :, :], cs[:, :, :], cT[:, :, :], ALU.mult))
            v.wait_ge(consts, 1)
            nc.vector.tensor_copy(cwide[:, :, :, :].rearrange("p l b q -> p (l b) q"),
                                  cs[:, :, :].rearrange("p l b -> p (l b)").unsqueeze(2).broadcast_to([P, 2 * B, QL]))\
                .then_inc(s_wx, 1)
            v.wait_ge(ld["v"], 64)
            own.count(nc.vector.tensor_reduce(wqkv1[:, 2, :], wv_raw, axis=AX.X, op=ALU.add))
            own.link(nc.vector.tensor_reduce(bqkv1[:, 2, :], bv_raw, axis=AX.X, op=ALU.add))
            v.wait_ge(s_modc, 2 * PAIRS)
            for j in (1, 4):
                mj = modb[:, :, :, j, :].rearrange("p l r d -> p (l r) d")
                own.count(nc.vector.tensor_scalar(mj, mj, 1.0, None, ALU.add))
            sgn = Zb[:, :, :]
            mag = Hb[:, :, :]
            for j in (2, 5):
                mj = modb[:, :, :, j, :].rearrange("p l r d -> p (l r) d")
                own.link(nc.vector.tensor_scalar(sgn, mj, 0.0, 2.0, ALU.is_ge, ALU.mult))
                own.link(nc.vector.tensor_scalar(mag, mj, -1.0, None, ALU.mult))
                own.link(nc.vector.tensor_tensor(mag, mag, mj, ALU.max))
                own.link(nc.vector.tensor_scalar(mag, mag, 0.25, None, ALU.max))
                own.link(nc.vector.scalar_tensor_tensor(out=mj, in0=sgn, scalar=-1.0, in1=mag, op0=ALU.add, op1=ALU.mult))
            v.wait_ge(ld["bc"], 16)
            own.link(nc.vector.tensor_tensor(gbias[:, :, :], modb[:, 0, :, 2, :],
                                             bproj[:, :].unsqueeze(1).broadcast_to([P, PAIRS, D]), ALU.mult))
            own.link(nc.vector.memset(vx[:, :, :, D:132], 1.0))

            v.wait_ge(ld["x"], 16 * B)
            def norm_a(i):
                xt = tiles(X, i)
                if i:
                    v.wait_ge(a_tr, 2 * i)
                stats_and_normalise(v, own, lambda t: X[:, i * NT + t, :], Zb, i + (NB["A"] + 1))
                own.link(nc.vector.tensor_tensor(Zb[:, :, :], Zb[:, :, :], modrow(0, i, 1), ALU.mult))
                nc.vector.tensor_tensor(Hb[:, :, :], Zb[:, :, :], modrow(0, i, 0), ALU.add).then_inc(a_h, 1)
                own.count(nc.vector.tensor_tensor(xt, xt, gbias[:, i, :].unsqueeze(1).broadcast_to([P, NT, D]), ALU.add))

            norm_a(0)
            for i in range(PAIRS):
                xt = tiles(X, i)
                for bb in range(2):
                    sl = slice(S * bb, S * bb + S)
                    v.wait_ge(a_act, i * 4 + (bb + 1))
                    own.count(nc.vector.scalar_tensor_tensor(out=phiq[:, sl], in0=hq_e[:, sl], scalar=1.0,
                                                             in1=hq_r[:, sl], op0=ALU.min, op1=ALU.add))
                for bb in range(2):
                    v.wait_ge(a_act, i * 4 + (bb + 3))
                    nc.vector.scalar_tensor_tensor(out=phik[:, bb], in0=k_e[:, bb], scalar=1.0,
                                                   in1=k_r[:, bb], op0=ALU.min, op1=ALU.add).then_inc(a_phi, 1)
                if i + 1 < PAIRS:
                    norm_a(i + 1)
                for bb in range(2):
                    v.wait_ge(a_kvx, i * 2 + (bb + 1))
                    nc.vector.tensor_tensor(kvb[:, bb, 0:D], bank(bb)[:, 0:D], blockmask[:, 0:D], ALU.mult)
                    nc.vector.tensor_scalar(kvb[:, bb, D:KX], blockmask[:, D:KX], bank(bb)[:, D:D + 1], None,
                                            ALU.mult).then_inc(a_kvb, 1)
                for bb in range(2):
                    v.wait_ge(a_num, i * 2 + (bb + 1))
                    num = bank(4 + 2 * bb, 2).rearrange("p (c n) -> p c n", c=NC)
                    own.link(nc.vector.tensor_scalar(rden[:, bb], num[:, :, D:KX], 1e-6, None, ALU.add))
                    own.link(nc.vector.reciprocal(rden[:, bb], rden[:, bb]))
                    for c in range(NC):
                        last = nc.vector.tensor_tensor(
                            oa[:, bb, c].rearrange("p (h e) -> p h e", h=H0),
                            num[:, c, 0:D].rearrange("p (h e) -> p h e", h=H0),
                            rden[:, bb, c].unsqueeze(2).broadcast_to([P, H0, DH0]), ALU.mult)
                    last.then_inc(a_o, 1)
                v.wait_ge(a_pr, i + 1)
                nc.vector.tensor_tensor(Zb[:, :, :], bank(2, 2).rearrange("p (t d) -> p t d", t=NT),
                                        modrow(0, i, 2), ALU.mult).then_inc(a_ga, 1)
                v.wait_ge(a_ga, i + 1)
                own.link(nc.vector.tensor_tensor(xt, xt, Zb[:, :, :], ALU.add))

            def norms_b(i):
                xt = tiles(X, i)
                stats_and_normalise(v, own, lambda t: X[:, i * NT + t, :], Zb, i * 2 + (NB["B"] + 1))
                own.link(nc.vector.tensor_tensor(Zb[:, :, :], Zb[:, :, :], modrow(0, i, 4), ALU.mult))
                own.link(nc.vector.tensor_tensor(Hb[:, :, :], Zb[:, :, :], modrow(0, i, 3), ALU.add))
                own.link(nc.vector.tensor_tensor(Zb[:, :, :], Hb[:, :, :], modrow(0, i, 5), ALU.mult))
                own.link(nc.vector.tensor_tensor(xt, xt, Zb[:, :, :], ALU.add))
                stats_and_normalise(v, own, lambda t: Hb[:, t, :], Zb, i * 2 + (NB["B"] + 2), b_z)

            def gates_b(i):
                g = dict(gw, g=gates[i % 2])
                v.wait_ge(b_lg, i + 1)
                lg = bank(0)[:, 0:NT * E].rearrange("p (t e) -> p t e", t=NT)
                own.link(nc.vector.tensor_reduce(g["m"], lg, axis=AX.X, op=ALU.max))
                nc.vector.tensor_tensor(g["l"], lg, over_experts(g["m"]), ALU.subtract).then_inc(b_l, 1)
                v.wait_ge(b_e, i + 1)
                own.link(nc.vector.tensor_reduce(g["s"], g["p"], axis=AX.X, op=ALU.add))
                own.link(nc.vector.reciprocal(g["s"], g["s"]))
                own.link(nc.vector.tensor_tensor(g["p"], g["p"], over_experts(g["s"]), ALU.mult))

                def first_of_largest(p, t, oh):
                    own.link(nc.vector.tensor_reduce(g[t], g[p], axis=AX.X, op=ALU.max))
                    own.link(nc.vector.tensor_tensor(g["w"], g[p], over_experts(g[t]), ALU.is_ge))
                    own.link(nc.vector.tensor_tensor(g["w"], g["w"], prio_b, ALU.mult))
                    own.link(nc.vector.tensor_reduce(g["m1"], g["w"], axis=AX.X, op=ALU.max))
                    own.link(nc.vector.tensor_tensor(g[oh], g["w"], over_experts(g["m1"]), ALU.is_equal))
                first_of_largest("p", "t1", "oh1")
                own.link(nc.vector.scalar_tensor_tensor(out=g["p2"], in0=g["oh1"], scalar=-4.0, in1=g["p"],
                                                        op0=ALU.mult, op1=ALU.add))
                first_of_largest("p2", "t2", "oh2")
                own.link(nc.vector.scalar_tensor_tensor(out=g["den"], in0=g["t1"], scalar=1e-9, in1=g["t2"],
                                                        op0=ALU.add, op1=ALU.add))
                own.link(nc.vector.reciprocal(g["rd"], g["den"]))
                own.count(nc.vector.tensor_tensor(g["c1"], g["t1"], g["rd"], ALU.mult))
                own.link(nc.vector.tensor_tensor(g["c2"], g["t2"], g["rd"], ALU.mult))
                own.count(nc.vector.tensor_tensor(g["oh1"], g["oh1"], over_experts(g["c1"]), ALU.mult))
                own.link(nc.vector.tensor_tensor(g["oh2"], g["oh2"], over_experts(g["c2"]), ALU.mult))
                nc.vector.tensor_tensor(g["g"], g["oh1"], g["oh2"], ALU.add).then_inc(b_g, 1)

            def turned_b(i):
                v.wait_ge(b_gT, i + 1)
                nc.vector.tensor_copy(gTs, bank(0, 2)[0:E, :]).then_inc(b_gTs, 1)

            norms_b(0)
            gates_b(0)
            turned_b(0)
            for i in range(PAIRS):
                xt = tiles(X, i)
                v.wait_ge(b_b2, i + 1)
                nc.vector.tensor_copy(acc, bank(0, 2).rearrange("p (t d) -> p t d", t=NT)).then_inc(b_ac0, 1)
                v.wait_ge(b_ac0, i + 1)
                for n in range(2 * E):
                    if i + 1 < PAIRS and n == 3:
                        norms_b(i + 1)
                    if i + 1 < PAIRS and n == 10:
                        gates_b(i + 1)
                    if i + 1 < PAIRS and n == 15:
                        turned_b(i + 1)
                    v.wait_ge(b_y, i * 16 + (n + 1))
                    for t in range(4):
                        tt = 4 * (n // E) + t
                        last = nc.vector.scalar_tensor_tensor(
                            out=acc[:, tt, :], in0=bank(2 + n % 2)[:, D * t:D * t + D],
                            scalar=gates[i % 2][:, tt, n % E:n % E + 1], in1=acc[:, tt, :], op0=ALU.mult, op1=ALU.add)
                    last.then_inc(b_ac, 1)
                    v.wait_ge(b_ac, i * 16 + (n + 1))
                own.link(nc.vector.tensor_tensor(acc, acc, modrow(0, i, 5), ALU.mult))
                own.link(nc.vector.tensor_tensor(xt, xt, acc, ALU.add))

            stage_c_vector(v, own)

            with v.Fori(0, PAIRS) as i:
                own.loop(i, "D")
                xt = tiles(X, i)
                g = gw
                stats_and_normalise(v, own, lambda t: X[:, i * NT + t, :], Zb, i + (NB["D"] + 1))
                own.link(nc.vector.tensor_tensor(Zb[:, :, :], Zb[:, :, :], modrow(1, i, 4), ALU.mult))
                nc.vector.tensor_tensor(Hb[:, :, :], Zb[:, :, :], modrow(1, i, 3), ALU.add).then_inc(d_h, 1)
                v.wait_ge(d_h, i + 1)
                v.wait_ge(d_lg, i + 1)
                lg = bank(2)[:, 0:NT * E].rearrange("p (t e) -> p t e", t=NT)
                own.link(nc.vector.tensor_reduce(g["m"], lg, axis=AX.X, op=ALU.max))
                own.link(nc.vector.tensor_tensor(g["w"], lg, over_experts(g["m"]), ALU.is_ge))
                own.link(nc.vector.tensor_tensor(g["w"], g["w"], prio_b, ALU.mult))
                own.link(nc.vector.tensor_reduce(g["m1"], g["w"], axis=AX.X, op=ALU.max))
                own.link(nc.vector.tensor_tensor(g["oh1"], g["w"], over_experts(g["m1"]), ALU.is_equal))
                for t2 in range(NT // 2):
                    for e2 in range(2):
                        n = 4 * t2 + 2 * e2
                        v.wait_ge(d_mm, i * 16 + (n + 2))
                        for e in range(4 * e2, 4 * e2 + 4):
                            for k in range(2):
                                t = 2 * t2 + k
                                own.count(nc.vector.scalar_tensor_tensor(
                                    out=Hb[:, t, :], in0=bank(4 + (n + k) % 4)[:, D * (e % 4):D * (e % 4) + D],
                                    scalar=g["oh1"][:, t, e:e + 1], in1=Hb[:, t, :], op0=ALU.mult, op1=ALU.add))
                                own.wait(1)
                        own.wait()
                        nc.vector.tensor_copy(dm2[:, :], half[:, 0:1]).then_inc(d_sel, 1)
                own.link(nc.vector.tensor_tensor(Hb[:, :, :], Hb[:, :, :], modrow(1, i, 5), ALU.mult))
                nc.vector.tensor_tensor(xt, xt, Hb[:, :, :], ALU.add).then_inc(d_x, 1)
            own.end(PAIRS)

        @block.tensor
        def _(pe):
            pe.wait_ge(consts, 1)
            pe.wait_ge(ld["w0"], 48)
            for t in range(3):
                nc.tensor.transpose(bank(4)[:, D * t:D * t + D], wqkv_raw[:, t, :], identf[:, :])
            nc.tensor.transpose(bank(4)[:, 3 * D:4 * D], wproj_raw[:, :], identf[:, :])
            for e in range(E):
                last = nc.tensor.transpose(bank(5, 2)[:, D * e:D * e + D], exp_raw[:, e, :], identf[:, :])
            last.then_inc(s_wT, 1)
            pe.wait_ge(s_wx, 1)
            pe.wait_ge(ld["mod"], 32)
            for n in range(2 * PAIRS):
                if n >= 2:
                    pe.wait_ge(s_modc, n - 1)
                l, r = n // PAIRS, n % PAIRS
                lhs = cwide[:, l, 2 * r:2 * r + 2, :].rearrange("p b q -> p (b q)")
                b = 2 * (n % 2)
                nc.tensor.matmul(bank(b), lhs, wmod[:, l, 0:512], start=True, stop=True)
                nc.tensor.matmul(bank(b + 1)[:, 0:256], lhs, wmod[:, l, 512:768], start=True, stop=True)\
                    .then_inc(s_mod, 1)
            pe.wait_ge(s_wTc, 3)
            pe.wait_ge(s_modc, 2 * PAIRS)

            for i in range(PAIRS):
                pe.wait_ge(a_h, i + 1)
                transpose_tiles(pe, Hb, a_tr)
                pe.wait_ge(a_hT, i * 2 + 2)
                if i:
                    pe.wait_ge(a_ga, i)
                for bb in range(2):
                    nc.tensor.matmul(bank(2 + bb), wqkvT[:, 0, :], xTb[:, bb, :], start=True, stop=True)\
                        .then_inc(a_q, 1)
                for bb in range(2):
                    for c in range(NC):
                        last = nc.tensor.matmul(bank(4 + 2 * bb, 2)[:, 256 * c:256 * c + 256],
                                                xTb[:, bb, P * c:P * c + P],
                                                wqkvT[:, 1:3, :].rearrange("p t d -> p (t d)"), start=True, stop=True)
                    last.then_inc(a_kv, 1)
                for bb in range(2):
                    pe.wait_ge(a_phi, i * 2 + (bb + 1))
                    for c in range(NC):
                        last = nc.tensor.matmul(bank(bb)[:, 0:D + 1], phik[:, bb, c, :], vx[:, bb, c, 0:D + 1],
                                                start=(c == 0), stop=(c == NC - 1))
                    last.then_inc(a_kvx, 1)
                for bb in range(2):
                    pe.wait_ge(a_kvb, i * 2 + (bb + 1))
                    for c in range(NC):
                        last = nc.tensor.matmul(bank(4 + 2 * bb, 2)[:, 256 * c:256 * c + KX],
                                                phiq[:, S * bb + P * c:S * bb + P * c + P], kvb[:, bb, :],
                                                start=True, stop=True)
                    last.then_inc(a_num, 1)
                for bb in range(2):
                    pe.wait_ge(a_o, i * 2 + (bb + 1))
                    for c in range(NC):
                        last = nc.tensor.transpose(bank(bb)[:, P * c:P * c + P], oa[:, bb, c, :], identf[:, :])
                    last.then_inc(a_oT, 1)
                pe.wait_ge(a_oTs, i * 2 + 2)
                for t in range(NT):
                    last = nc.tensor.matmul(bank(2 + t // 4)[:, D * (t % 4):D * (t % 4) + D], oaT[:, P * t:P * t + P], wprojT[:, :],
                                            start=True, stop=True)
                last.then_inc(a_pr, 1)

            pe.wait_ge(ld["wg"], 96)
            pe.wait_ge(ld["moe"], 64)
            def tokens_b(i):
                pe.wait_ge(b_z, i + 1)
                if i:
                    pe.wait_ge(b_ac0, i)
                transpose_tiles(pe, Zb, b_tr)

            def logits_b(i):
                pe.wait_ge(b_xT, i * 2 + 2)
                for t in range(NT):
                    last = nc.tensor.matmul(bank(0)[:, E * t:E * t + E], xTs[i % 2][:, P * t:P * t + P], wgT[:, :],
                                            start=True, stop=True)
                last.then_inc(b_lg, 1)

            def gates_t(i):
                pe.wait_ge(b_g, i + 1)
                for t in range(NT):
                    last = nc.tensor.transpose(bank(0, 2)[0:E, P * t:P * t + P], gates[i % 2][:, t, :], identf[:, :])
                last.then_inc(b_gT, 1)

            def bias_b(i):
                pe.wait_ge(b_gTs, i + 1)
                for t in range(NT):
                    last = nc.tensor.matmul(bank(0, 2)[:, D * t:D * t + D], gTs[:, P * t:P * t + P], b2r[:, :],
                                            start=True, stop=True)
                last.then_inc(b_b2, 1)

            tokens_b(0)
            logits_b(0)
            gates_t(0)
            bias_b(0)
            for i in range(PAIRS):
                def hidden(n):
                    for fc in range(FC):
                        if n:
                            pe.wait_ge(b_ge, i * 64 + (4 * (n - 1) + fc + 1))
                        nc.tensor.matmul(bank(4 + fc), W1[:, n % E, P * fc:P * fc + P],
                                         xTs[i % 2][:, 512 * (n // E):512 * (n // E) + 512], start=True, stop=True)\
                            .then_inc(b_mm, 1)

                def second(n):
                    pe.wait_ge(b_ge, i * 64 + 4 * (n + 1))
                    if i * 16 + n >= 2:
                        pe.wait_ge(b_ac, i * 16 + (n - 1))
                    for t in range(4):
                        for fc in range(FC):
                            last = nc.tensor.matmul(bank(2 + n % 2)[:, D * t:D * t + D],
                                                    hid[:, n % 2, fc, P * t:P * t + P], W2[:, n % E, fc, :],
                                                    start=(fc == 0), stop=(fc == FC - 1))
                    last.then_inc(b_y, 1)
                for n in range(2 * E):
                    hidden(n)
                    if n:
                        second(n - 1)
                    if i + 1 < PAIRS:
                        for at, part in ((8, tokens_b), (10, logits_b), (14, gates_t)):
                            if n == at:
                                part(i + 1)
                second(2 * E - 1)
                if i + 1 < PAIRS:
                    bias_b(i + 1)

            pe.wait_ge(ld["w1"], 32)
            stage_c_tensor(pe)

            with pe.Fori(0, PAIRS) as i:
                pe.wait_ge(d_h, i + 1)
                transpose_tiles(pe, Hb, d_tr)
                pe.wait_ge(d_hT, i * 2 + 2)
                for t in range(NT):
                    last = nc.tensor.matmul(bank(2)[:, E * t:E * t + E], xT[:, P * t:P * t + P], gateT[:, :],
                                            start=True, stop=True)
                last.then_inc(d_lg, 1)
                for n in range(2 * NT):
                    t, e2 = 2 * (n // 4) + n % 2, n // 2 % 2
                    if n >= 4:
                        pe.wait_ge(d_sel, i * NT + (n // 2 - 1))
                    nc.tensor.matmul(bank(4 + n % 4), xT[:, P * t:P * t + P],
                                     expT[:, 4 * e2:4 * e2 + 4, :].rearrange("p e d -> p (e d)"),
                                     start=True, stop=True).then_inc(d_mm, 1)



_INS = ['L0_attn_x', 'L0_attn_w_qkv', 'L0_attn_w_proj', 'L0_attn_b_proj', 'L0_ffn_gamma', 'L0_ffn_beta', 'L0_ffn_Wg',
        'L0_ffn_W1', 'L0_ffn_b1', 'L0_ffn_W2', 'L0_ffn_b2', 'L0_c', 'L0_wmod', 'L1_attn_Wq', 'L1_attn_bq', 'L1_attn_Wk',
        'L1_attn_bk', 'L1_attn_Wv', 'L1_attn_bv', 'L1_attn_gamma', 'L1_attn_beta', 'L1_ffn_gate_w', 'L1_ffn_expert_w',
        'L1_c', 'L1_wmod']


def kernel(**inputs):
    import numpy as _np
    import concourse.bacc as _bacc
    from concourse import mybir as _mybir
    from concourse.bass_utils import run_bass_kernel_spmd as _run

    nc = _bacc.Bacc("TRN2", target_bir_lowering=False, num_devices=1)
    arrays, io = {}, {}
    for name in _INS:
        a = _np.ascontiguousarray(inputs[name])
        arrays[f"in_{name}_dram"] = a
        io[name] = nc.dram_tensor(f"in_{name}_dram", a.shape, _mybir.dt.from_np(a.dtype), kind="ExternalInput").ap()
    out = nc.dram_tensor("out_0_dram", (B, S, D), _mybir.dt.float32, kind="ExternalOutput").ap()
    build(nc, io, out)
    r = _run(nc, [arrays], core_ids=[0])
    return r.results[0]["out_0_dram"]
```
